# Optimizing a Trainium2 kernel written in Bass

```python
import numpy as np
import jax
import jax.numpy as jnp

def _softmax(x, axis=-1):
    return jax.nn.softmax(x, axis=axis)

def _gelu(x):
    return jax.nn.gelu(x, approximate=True)

def _silu(x):
    return jax.nn.silu(x)

def _sigmoid(x):
    return jax.nn.sigmoid(x)

def _layernorm(x, axis=-1, eps=1e-05):
    m = jnp.mean(x, axis=axis, keepdims=True)
    v = jnp.var(x, axis=axis, keepdims=True)
    return (x - m) / jnp.sqrt(v + eps)

def _scatter_add(tgt, idx, src, axis=0):
    return tgt.at[idx].add(src)

def _segment_sum(src, seg, n):
    return jax.ops.segment_sum(src, seg, n)
kernel_name = 'mk_xattn_seq_d1_seqx_r4_c5e457'

def setup_inputs(seed: int=0):
    np.random.seed(seed)
    _w = jnp.asarray

    def _rec_inputs():
        import jax
        import jax.numpy as jnp
        _rk = jax.random.key(seed)
        x = 7.22e-05 + 1 * jax.random.normal(jax.random.fold_in(_rk, 1), (4, 512, 512), jnp.float32)
        _lenS = 512 - jax.random.randint(jax.random.fold_in(_rk, 7), (4,), 0, max(1, 512 // 4) + 1, jnp.int32)
        _lenS2 = 64 - jax.random.randint(jax.random.fold_in(_rk, 8), (4,), 0, max(1, 64 // 4) + 1, jnp.int32)
        _ctx_2048P = jax.random.normal(jax.random.fold_in(_rk, 11), (4, 16, 512), jnp.float32)
        _ctx_2048c = jax.random.dirichlet(jax.random.fold_in(_rk, 511), 0.3 * jnp.ones((16,), jnp.float32), (4, 64))
        _ctx_2048t = jnp.einsum('bsk,bkd->bsd', _ctx_2048c, _ctx_2048P)
        _ctx_2048t = _ctx_2048t * jax.lax.rsqrt(jnp.mean(jnp.square(_ctx_2048t)) + 1e-12) * 0.953939
        ctx_2048 = 4.13588e-05 + 0.999923 * (_ctx_2048t + 0.3 * jax.random.normal(jax.random.fold_in(_rk, 611), (4, 64, 512), jnp.float32))
        _validS = jnp.arange(512)[None, :] < _lenS[:, None]
        _validS2 = jnp.arange(64)[None, :] < _lenS2[:, None]
        _causal = jnp.tril(jnp.ones((512, 512), dtype=bool))
        mask_Bx1xSxS2_ff0 = jnp.where(jnp.ones((4, 1, 512, 64), dtype=bool), 0.0, -1000000000.0).astype(jnp.float32)
        return (x, ctx_2048, mask_Bx1xSxS2_ff0)
    x, ctx_2048, mask_Bx1xSxS2_ff0 = _rec_inputs()

    def _L0_xattn_setup():
        import jax, jax.numpy as jnp
        import numpy as np
        H = 512
        NH = 32
        KVH = 8
        HD = H // NH
        GROUPS = NH // KVH
        EPS = 1e-06
        B, L, S = (4, 256, 256)

        def _gqa_forward(hidden_state, encoder_hidden_state, encoder_attention_mask, Wq, bq, Wk, bk, Wv, bv, Wo, bo, gamma, beta):
            b, l, _ = hidden_state.shape
            s = encoder_hidden_state.shape[1]
            q = hidden_state @ Wq + bq
            k = encoder_hidden_state @ Wk + bk
            v = encoder_hidden_state @ Wv + bv
            q = q.reshape(b, l, KVH, GROUPS, HD).transpose(0, 2, 3, 1, 4)
            k = k.reshape(b, s, KVH, HD).transpose(0, 2, 1, 3)
            v = v.reshape(b, s, KVH, HD).transpose(0, 2, 1, 3)
            scale = 1.0 / jnp.sqrt(jnp.asarray(HD, q.dtype))
            scores = jnp.einsum('bkgld,bksd->bkgls', q, k) * scale
            scores = scores + encoder_attention_mask[:, :, None, :, :]
            attn = jax.nn.softmax(scores, axis=-1)
            out = jnp.einsum('bkgls,bksd->bkgld', attn, v)
            out = out.transpose(0, 3, 1, 2, 4).reshape(b, l, H)
            out = out @ Wo + bo
            x = out + hidden_state
            mu = jnp.mean(x, axis=-1, keepdims=True)
            var = jnp.var(x, axis=-1, keepdims=True)
            return (x - mu) * jax.lax.rsqrt(var + EPS) * gamma + beta
        key = jax.random.key(seed)
        ks = jax.random.split(key, 12)
        sd = 0.02
        return {'hidden_state': jax.random.normal(ks[0], (B, L, H), jnp.float32), 'encoder_hidden_state': jax.random.normal(ks[1], (B, S, H), jnp.float32), 'encoder_attention_mask': jnp.zeros((B, 1, L, S), jnp.float32), 'Wq': jax.random.normal(ks[2], (H, H), jnp.float32) * sd, 'bq': jnp.zeros((H,), jnp.float32), 'Wk': jax.random.normal(ks[3], (H, KVH * HD), jnp.float32) * sd, 'bk': jnp.zeros((KVH * HD,), jnp.float32), 'Wv': jax.random.normal(ks[4], (H, KVH * HD), jnp.float32) * sd, 'bv': jnp.zeros((KVH * HD,), jnp.float32), 'Wo': jax.random.normal(ks[5], (H, H), jnp.float32) * sd, 'bo': jnp.zeros((H,), jnp.float32), 'gamma': jnp.ones((H,), jnp.float32), 'beta': jnp.zeros((H,), jnp.float32)}
    _L0_xattn_all = _L0_xattn_setup()
    _L0_xattn_in = {k: v for k, v in _L0_xattn_all.items() if k in ('Wq', 'bq', 'Wk', 'bk', 'Wv', 'bv', 'Wo', 'bo', 'gamma', 'beta')}
    del _L0_xattn_all
    return {'x': x, 'ctx_2048': ctx_2048, 'mask_Bx1xSxS2_ff0': mask_Bx1xSxS2_ff0, 'L0_xattn_Wq': _L0_xattn_in['Wq'], 'L0_xattn_bq': _L0_xattn_in['bq'], 'L0_xattn_Wk': _L0_xattn_in['Wk'], 'L0_xattn_bk': _L0_xattn_in['bk'], 'L0_xattn_Wv': _L0_xattn_in['Wv'], 'L0_xattn_bv': _L0_xattn_in['bv'], 'L0_xattn_Wo': _L0_xattn_in['Wo'], 'L0_xattn_bo': _L0_xattn_in['bo'], 'L0_xattn_gamma': _L0_xattn_in['gamma'], 'L0_xattn_beta': _L0_xattn_in['beta']}

def reference(x, ctx_2048, mask_Bx1xSxS2_ff0, L0_xattn_Wq, L0_xattn_bq, L0_xattn_Wk, L0_xattn_bk, L0_xattn_Wv, L0_xattn_bv, L0_xattn_Wo, L0_xattn_bo, L0_xattn_gamma, L0_xattn_beta):
    import jax
    import jax.numpy as jnp

    def _L0_xattn_ref(hidden_state, encoder_hidden_state, encoder_attention_mask, Wq, bq, Wk, bk, Wv, bv, Wo, bo, gamma, beta):
        import jax, jax.numpy as jnp
        import numpy as np
        H = 512
        NH = 32
        KVH = 8
        HD = H // NH
        GROUPS = NH // KVH
        EPS = 1e-06
        B, L, S = (4, 256, 256)

        def _gqa_forward(hidden_state, encoder_hidden_state, encoder_attention_mask, Wq, bq, Wk, bk, Wv, bv, Wo, bo, gamma, beta):
            b, l, _ = hidden_state.shape
            s = encoder_hidden_state.shape[1]
            q = hidden_state @ Wq + bq
            k = encoder_hidden_state @ Wk + bk
            v = encoder_hidden_state @ Wv + bv
            q = q.reshape(b, l, KVH, GROUPS, HD).transpose(0, 2, 3, 1, 4)
            k = k.reshape(b, s, KVH, HD).transpose(0, 2, 1, 3)
            v = v.reshape(b, s, KVH, HD).transpose(0, 2, 1, 3)
            scale = 1.0 / jnp.sqrt(jnp.asarray(HD, q.dtype))
            scores = jnp.einsum('bkgld,bksd->bkgls', q, k) * scale
            scores = scores + encoder_attention_mask[:, :, None, :, :]
            attn = jax.nn.softmax(scores, axis=-1)
            out = jnp.einsum('bkgls,bksd->bkgld', attn, v)
            out = out.transpose(0, 3, 1, 2, 4).reshape(b, l, H)
            out = out @ Wo + bo
            x = out + hidden_state
            mu = jnp.mean(x, axis=-1, keepdims=True)
            var = jnp.var(x, axis=-1, keepdims=True)
            return (x - mu) * jax.lax.rsqrt(var + EPS) * gamma + beta
        return _gqa_forward(hidden_state, encoder_hidden_state, encoder_attention_mask, Wq, bq, Wk, bk, Wv, bv, Wo, bo, gamma, beta)
    x = _L0_xattn_ref(x, ctx_2048, mask_Bx1xSxS2_ff0, L0_xattn_Wq, L0_xattn_bq, L0_xattn_Wk, L0_xattn_bk, L0_xattn_Wv, L0_xattn_bv, L0_xattn_Wo, L0_xattn_bo, L0_xattn_gamma, L0_xattn_beta)
    return x

_drawn_inputs = setup_inputs


def setup_inputs(seed=0):
    import zlib

    import numpy as np

    out = dict(_drawn_inputs(seed))
    spreads = {'L0_xattn_bq': (0.0, 0.8),
     'L0_xattn_bk': (0.0, 0.8),
     'L0_xattn_bv': (0.0, 0.1),
     'L0_xattn_bo': (0.0, 0.1),
     'L0_xattn_gamma': (1.0, 0.2),
     'L0_xattn_beta': (0.0, 0.1)}
    factors = {'L0_xattn_Wq': 6.805, 'L0_xattn_Wk': 6.742}
    for name, (base, spread) in spreads.items():
        noise = np.random.default_rng([zlib.crc32(name.encode()), seed]).standard_normal(out[name].shape)
        drawn = base * np.exp(spread * noise) if base else spread * noise
        out[name] = jnp.asarray(drawn.astype(out[name].dtype))
    for name, factor in factors.items():
        out[name] = (out[name] * factor).astype(out[name].dtype)
    return out
```

```python
from contextlib import ExitStack

import numpy as np

import concourse.bass as bass
from concourse import mybir

ALU = mybir.AluOpType
ACT = mybir.ActivationFunctionType
AX = mybir.AxisListType
F32 = mybir.dt.float32
F32R = mybir.dt.float32r
BF16 = mybir.dt.bfloat16

P = 128
B, L, S, D = 4, 512, 64, 512
NH, KVH = 32, 8
HD = D // NH
NC = D // P
HPC = NH // NC
KPC = KVH // NC
PAIRS = HPC // 2
GRP = NH // KVH
BLK = 32
NB = L // BLK
EPS = 1e-6
SCALE = 0.25

C_MASK, C_SPREAD = 0, P
C_ROUNDED = C_SPREAD + NC * P
C_ID, C_MAX = C_ROUNDED, C_ROUNDED + P
C_SUM = C_MAX + 2 * P
C_HEAD = C_SUM + NC * BLK
C_HALF = C_HEAD + GRP
C_ALL = C_HALF + 2

ITEMS = ["Q1", "Q2", "R0", "R1", "R2", "R3", "Q3", "O0", "O1", "O2", "O3", "Q0"]


def item(b, name, tail, last=False):
    if last:
        return 12 * B - 8 + ["R0", "R1", "R2", "R3", "O0", "O1", "O2", "O3"].index(name)
    if not tail:
        return ["Q1", "Q2", "Q3", "Q0"].index(name) + 1
    return 12 * b - 7 + ITEMS.index(name)


def bank_of(name, tail, last=False):
    return item(1, name, tail, last) % 2


def cross_attention(nc, x_t, x_n, ctx_t, mask_t, wq, bq, wk, bk, wv, bv, wo, bo, gamma, beta, consts, out):
    with ExitStack() as ctx:
        def sb(name, shape, dt=F32):
            return ctx.enter_context(nc.sbuf_tensor(name, shape, dt))

        def sem(name):
            return ctx.enter_context(nc.semaphore(name))

        const = sb("const", [P, C_ALL])
        const_r = sb("const_r", [P, C_ROUNDED], F32R)
        ctx_sb = sb("ctx_sb", [P, NC, B * S])
        wk_sb = sb("wk_sb", [P, NC, P])
        wv_sb = sb("wv_sb", [P, NC, P])
        bq_sb = sb("bq_sb", [P, NC])
        bk_sb = sb("bk_sb", [P, 1])
        bv_sb = sb("bv_sb", [P, P])
        bo_sb = sb("bo_sb", [P, D])
        gamma_sb = sb("gamma_sb", [P, D])
        beta_sb = sb("beta_sb", [P, D])
        wq_hi = sb("wq_hi", [P, NC, D], F32R)
        wq_lo = sb("wq_lo", [P, NC, D], F32R)
        wo_hi = sb("wo_hi", [P, NC, D], F32R)
        wo_lo = sb("wo_lo", [P, NC, D], F32R)
        xt_raw = sb("xt_raw", [P, NC, L])
        x_hi = sb("x_hi", [P, NC, L], F32R)
        x_lo = sb("x_lo", [P, NC, L], F32R)
        kt = sb("kt", [P, B * S])
        kt_hi = sb("kt_hi", [P, B * S], F32R)
        kt_lo = sb("kt_lo", [P, B * S], F32R)
        k_rep = sb("k_rep", [P, B, 2, KVH, S])
        k_blk = sb("k_blk", [P, 2, KVH, GRP, S], F32R)
        v_rows = sb("v_rows", [P, B, P])
        v_blk = sb("v_blk", [P, KVH, 2, HD])
        mask_raw = sb("mask_raw", [P, L])
        mask_rnd = sb("mask_rnd", [P, L], F32R)
        mask_parts = sb("mask_parts", [P, L], F32R)
        q_parts = sb("q_parts", [P, 2, 2, L], F32R)
        blk_max = sb("blk_max", [P, 2, 2 * NB])
        oth_max = sb("oth_max", [P, 2, 2 * NB])
        tok_max = sb("tok_max", [P, 2, 2 * NB])
        max_rest = sb("max_rest", [P, 2, 2 * NB])
        max_cols = sb("max_cols", [P, 2, NB, BLK], BF16)
        max_rows = sb("max_rows", [P, 2, L], BF16)
        neg_pick = sb("neg_pick", [P, 2 * P], BF16)
        probs = sb("probs", [P, 2, PAIRS, L])
        o_raw = sb("o_raw", [P, NC, L])
        rsum = sb("rsum", [P, L])
        rsum_hi = sb("rsum_hi", [P, L], F32R)
        rsum_lo = sb("rsum_lo", [P, L], F32R)
        o_norm = sb("o_norm", [P, 2, L])
        o_hi = sb("o_hi", [P, NC, L], F32R)
        o_lo = sb("o_lo", [P, NC, L], F32R)
        res_x = sb("res_x", [P, NC, D])
        y = sb("y", [P, NC, D])
        stats = sb("stats", [P, NC, 6])
        mean_var = sb("mean_var", [P, NC, 2])
        var_eps = sb("var_eps", [P, NC])
        rstd = sb("rstd", [P, NC])
        eps = sb("eps", [P, 1])
        neg_half = sb("neg_half", [P, 1])

        ps_s = ctx.enter_context(nc.psum_tensor("ps_s", [P, PAIRS, L], F32))
        ps_o = ctx.enter_context(nc.psum_tensor("ps_o", [P, L], F32))
        ps_z = ctx.enter_context(nc.psum_tensor("ps_z", [P, L], F32))
        ps_w = ctx.enter_context(nc.psum_tensor("ps_w", [P, 2, L], F32))

        k_in = sem("k_in")
        v_in = sem("v_in")
        vec_in = sem("vec_in")
        y_dma = [sem(f"y_dma{t}") for t in range(NC)]
        res_in = [sem(f"res_in{t}") for t in range(NC)]
        x_in = [sem(f"x_in{k}") for k in range(NC)]
        mask_in = sem("mask_in")
        zeroed = sem("zeroed")
        const_rounded = sem("const_rounded")
        kt_done = sem("kt_done")
        kt_added = sem("kt_added")
        kt_split = sem("kt_split")
        rep_done = sem("rep_done")
        rep_copied_a = sem("rep_copied_a")
        rep_copied_d = sem("rep_copied_d")
        v_done = sem("v_done")
        v_copied = sem("v_copied")
        wq_hi_ready = sem("wq_hi_ready")
        wq_lo_ready = sem("wq_lo_ready")
        wo_hi_ready = sem("wo_hi_ready")
        wo_lo_ready = sem("wo_lo_ready")
        x_hi_ready = sem("x_hi_ready")
        x_lo_ready = sem("x_lo_ready")
        k_ready = sem("k_ready")
        v_ready = sem("v_ready")
        mask_rounded = sem("mask_rounded")
        mask_ready = sem("mask_ready")
        scores_done = sem("scores_done")
        max_done = sem("max_done")
        oth_copied = sem("oth_copied")
        tok_max_done = sem("tok_max_done")
        max_top_done = sem("max_top_done")
        max_rest_done = sem("max_rest_done")
        max_mid_done = sem("max_mid_done")
        max_low_done = sem("max_low_done")
        max_ready = sem("max_ready")
        shifted = sem("shifted")
        exp_done = sem("exp_done")
        pv_done = sem("pv_done")
        o_copied = sem("o_copied")
        z_read = sem("z_read")
        rsum_hi_done = sem("rsum_hi_done")
        rsum_ready = sem("rsum_ready")
        item_done = sem("item_done")
        q_read = sem("q_read")
        q_hi_done = sem("q_hi_done")
        norm_done = sem("norm_done")
        o_hi_ready = sem("o_hi_ready")
        o_lo_ready = sem("o_lo_ready")
        res_ready = sem("res_ready")
        resid_done = sem("resid_done")
        stats_done = sem("stats_done")
        mean_done = sem("mean_done")
        gamma_done = sem("gamma_done")
        eps_done = sem("eps_done")
        rstd_done = sem("rstd_done")
        scaled = sem("scaled")
        y_ready = sem("y_ready")

        pick = k_blk[:, 0, 0:KVH // 2, :, :].rearrange("p h g s -> p (h g s)")

        block = ctx.enter_context(nc.Block())

        def row(a):
            return a.rearrange("(o n) -> o n", o=1)

        @block.sync
        def _(sp):
            sp.dma_start(const[:], consts).then_inc(k_in, 16)
            sp.dma_start(ctx_sb[:], ctx_t).then_inc(k_in, 16)
            sp.dma_start(bk_sb[:], bk).then_inc(k_in, 16)
            sp.dma_start(bq_sb[:], bq).then_inc(vec_in, 16)
            for k in range(NC):
                sp.dma_start(xt_raw[:, k, :], x_t[0, k]).then_inc(x_in[k], 16)
            for h in range(2):
                sp.dma_start(mask_raw[h * S:(h + 1) * S, :], mask_t[0]).then_inc(mask_in, 16)
            sp.dma_start(bo_sb[:], row(bo).broadcast_to([P, D])).then_inc(vec_in, 16)
            sp.dma_start(gamma_sb[:], row(gamma).broadcast_to([P, D])).then_inc(vec_in, 16)
            sp.dma_start(beta_sb[:], row(beta).broadcast_to([P, D])).then_inc(vec_in, 16)
            for t in range(NC):
                sp.dma_start(res_x[:, t, :], wo[t * P:(t + 1) * P, :]).then_inc(res_in[t], 16)

            def store(bt, t):
                sp.wait_ge(y_ready, 4 * bt + t + 1)
                sp.dma_start(out[bass.ds((bt * NC + t) * P, P), :], y[:, t, :]).then_inc(y_dma[t], 16)

            def batch(b, tail, nxt):
                if nxt:
                    sp.wait_ge(x_lo_ready, 4 * b + 4)
                    for k in range(NC):
                        sp.dma_start(xt_raw[:, k, :], x_t[b + 1, k] if isinstance(b, int) else
                                     x_t[bass.ds(b + 1, 1), k].rearrange("o p n -> (o p) n")).then_inc(x_in[k], 16)
                    sp.wait_ge(mask_ready, b + 1)
                    for h in range(2):
                        sp.dma_start(mask_raw[h * S:(h + 1) * S, :], mask_t[b + 1] if isinstance(b, int) else
                                     mask_t[bass.ds(b + 1, 1)].rearrange("o p n -> (o p) n")).then_inc(mask_in, 16)
                for t in range(NC):
                    if tail:
                        sp.wait_ge(resid_done, 4 * b - 4 + t + 1)
                    else:
                        sp.wait_ge(wo_lo_ready, t + 1)
                    sp.dma_start(res_x[:, t, :], x_n[bass.ds((b * NC + t) * P, P), :]).then_inc(res_in[t], 16)
                    if tail:
                        store(b - 1, t)

            batch(0, tail=False, nxt=True)
            with sp.Fori(1, B - 1) as b:
                batch(b, tail=True, nxt=True)
            batch(B - 1, tail=True, nxt=False)
            for t in range(NC):
                store(B - 1, t)
            for t in range(NC):
                sp.wait_ge(y_dma[t], 16 * (B + 1))

        @block.tensor
        def _(pe):
            mm = nc.tensor.matmul

            def q_item(b, c, bank, free=None):
                if c == 0 and not isinstance(b, int):
                    pe.wait_ge(x_lo_ready, 4 * b + 4)
                dst = ps_w[:, bank, :]
                if free:
                    pe.wait_ge(*free)
                for k in range(NC):
                    if c == 0 and isinstance(b, int):
                        if b == 0:
                            pe.wait_ge(wq_lo_ready, k + 1)
                        pe.wait_ge(x_lo_ready, 4 * b + k + 1)
                    wh = wq_hi[:, k, c * P:(c + 1) * P]
                    wl = wq_lo[:, k, c * P:(c + 1) * P]
                    mm(dst, wh, x_hi[:, k, :], start=k == 0, stop=False)
                    mm(dst, wh, x_lo[:, k, :], start=False, stop=False)
                    last = mm(dst, wl, x_hi[:, k, :], start=False, stop=k == NC - 1)
                last.then_inc(item_done, 1)

            def spread_item(bt, c, bank, free=None):
                pe.wait_ge(rsum_ready, bt + 1)
                if free:
                    pe.wait_ge(*free)
                sel = const_r[:, C_SPREAD + c * P:C_SPREAD + (c + 1) * P]
                mm(ps_w[:, bank, :], sel, rsum_hi[:], start=True, stop=False)
                mm(ps_w[:, bank, :], sel, rsum_lo[:], start=False, stop=True).then_inc(item_done, 1)

            def out_item(bt, t, bank, free=None):
                if free:
                    pe.wait_ge(*free)
                pe.wait_ge(o_lo_ready, 4 * bt + 4)
                for c in range(NC):
                    oh = o_hi[:, c, t * P:(t + 1) * P]
                    ol = o_lo[:, c, t * P:(t + 1) * P]
                    mm(ps_w[:, bank, :], oh, wo_hi[:, c, :], start=c == 0, stop=False)
                    mm(ps_w[:, bank, :], oh, wo_lo[:, c, :], start=False, stop=False)
                    last = mm(ps_w[:, bank, :], ol, wo_hi[:, c, :], start=False, stop=c == NC - 1)
                last.then_inc(item_done, 1)

            def scores(b, c):
                i = 4 * b + c
                pe.wait_ge(q_read, i + 1)
                pe.wait_ge(k_ready, i + 1)
                if c == 0:
                    pe.wait_ge(mask_ready, b + 1)
                for j in range(PAIRS):
                    if j % 2 == 0 and not (isinstance(i, int) and i == 0):
                        pe.wait_ge(exp_done, 2 * i - 1 + j // 2)
                    kv, g = KPC * c + j // 2, 2 * (j % 2)
                    q = q_parts[:, c % 2, j // 2, :]
                    mm(ps_s[:, j, :], k_blk[:, 0, kv, g:g + 2, :], q, start=True, stop=False, skip_group_check=True)
                    mm(ps_s[:, j, :], k_blk[:, 1, kv, g:g + 2, :], q, start=False, stop=False, skip_group_check=True)
                    last = mm(ps_s[:, j, :], const_r[:, C_MASK:C_MASK + P], mask_parts[:],
                              start=False, stop=True, skip_group_check=True)
                    if j % 2 == 1:
                        last.then_inc(scores_done, 1)

            def shift(b, c):
                for g in range(2):
                    pe.wait_ge(max_ready, 2 * (4 * b + c) + g + 1)
                    for j in range(2):
                        last = mm(ps_s[:, 2 * g + j, :], neg_pick[:, j * P:(j + 1) * P],
                                  max_rows[:, g, :], start=False, stop=True, skip_group_check=True)
                    last.then_inc(shifted, 1)

            def values(b, c):
                i = 4 * b + c
                pe.wait_ge(exp_done, 2 * i + 2)
                if not (isinstance(i, int) and i == 0):
                    pe.wait_ge(o_copied, i)
                if c == 0:
                    pe.wait_ge(v_ready, b + 1)
                    if not isinstance(b, int) or b > 0:
                        pe.wait_ge(z_read, b)
                for j in range(PAIRS):
                    mm(ps_o[BLK * j:BLK * (j + 1), :], v_blk[:, KPC * c + j // 2, :, :], probs[:, c % 2, j, :],
                       start=True, stop=True)
                for j in range(PAIRS):
                    last = mm(ps_z[BLK * j:BLK * (j + 1), :], const[:, C_SUM + c * BLK:C_SUM + (c + 1) * BLK],
                              probs[:, c % 2, j, :], start=c == 0, stop=c == NC - 1, skip_group_check=True)
                last.then_inc(pv_done, 1)

            pe.wait_ge(k_in, 4 * 16)
            for k in range(NC):
                last = mm(ps_o[:, 0:B * S], wk_sb[:, k, :], ctx_sb[:, k, :], start=k == 0, stop=k == NC - 1)
            last.then_inc(kt_done, 1)
            pe.wait_ge(v_in, 16)
            for b in range(B):
                for k in range(NC):
                    for h in range(2):
                        last = mm(ps_z[h * S:(h + 1) * S, b * P:(b + 1) * P], ctx_sb[:, k, b * S:(b + 1) * S],
                                  wv_sb[:, k, :], start=k == 0, stop=k == NC - 1)
            last.then_inc(v_done, 1)
            pe.wait_ge(const_rounded, 1)
            for part, parts in enumerate((kt_hi, kt_lo)):
                pe.wait_ge(kt_split, part + 1)
                if part:
                    pe.wait_ge(rep_copied_a, 1)
                    pe.wait_ge(rep_copied_d, 1)
                for kv in range(KVH):
                    last = mm(ps_s[:, kv // 2, (kv % 2) * B * S:(kv % 2 + 1) * B * S],
                              pick[:, kv * P:(kv + 1) * P], parts[:],
                              start=True, stop=True)
                last.then_inc(rep_done, 1)
            q_item(0, 0, 0)
            pe.wait_ge(rep_copied_a, 2)
            pe.wait_ge(rep_copied_d, 2)

            def batch(b, tail, nxt):
                def bank(name):
                    return bank_of(name, tail)
                bt = b - 1
                scores(b, 0)
                q_item(b, 1, bank("Q1"))
                shift(b, 0)
                if tail:
                    values(bt, NC - 1)
                scores(b, 1)
                q_item(b, 2, bank("Q2"))
                if tail:
                    spread_item(bt, 0, bank("R0"))
                shift(b, 1)
                values(b, 0)
                if tail:
                    spread_item(bt, 1, bank("R1"), (q_read, 4 * b + 3))
                    spread_item(bt, 2, bank("R2"), (norm_done, 4 * bt + 1))
                    spread_item(bt, 3, bank("R3"), (norm_done, 4 * bt + 2))
                scores(b, 2)
                q_item(b, 3, bank("Q3"), (norm_done, 4 * bt + 3) if tail else None)
                if tail:
                    out_item(bt, 0, bank("O0"))
                shift(b, 2)
                values(b, 1)
                if tail:
                    out_item(bt, 1, bank("O1"), (q_read, 4 * b + 4))
                scores(b, 3)
                if tail:
                    out_item(bt, 2, bank("O2"), (resid_done, 4 * bt + 1))
                shift(b, 3)
                values(b, 2)
                if tail:
                    out_item(bt, 3, bank("O3"), (resid_done, 4 * bt + 2))
                if nxt:
                    q_item(b + 1, 0, bank("Q0"), (resid_done, 4 * bt + 3) if tail else None)

            batch(0, tail=False, nxt=True)
            pe.wait_ge(wo_lo_ready, NC)
            with pe.Fori(1, B - 1) as b:
                batch(b, tail=True, nxt=True)
            batch(B - 1, tail=True, nxt=False)
            bt = B - 1
            values(bt, NC - 1)
            for c in range(NC):
                spread_item(bt, c, bank_of(f"R{c}", True, True),
                            (resid_done, 4 * bt - 1 + c) if c < 2 else (norm_done, 4 * bt - 1 + c))
            for t in range(NC):
                out_item(bt, t, bank_of(f"O{t}", True, True), (resid_done, 4 * bt - 1 + t) if t >= 2 else None)

        @block.scalar
        def _(act):
            act.dma_start(wk_sb[:], wk.rearrange("(k p) n -> p k n", p=P)).then_inc(k_in, 16)
            for k in range(NC):
                act.dma_start(y[:, k, :], wq[k * P:(k + 1) * P, :]).then_inc(y_dma[k], 16)
            act.dma_start(wv_sb[:], wv.rearrange("(k p) n -> p k n", p=P)).then_inc(v_in, 16)
            act.dma_start(bv_sb[:], row(bv).broadcast_to([P, P])).then_inc(vec_in, 16)
            go = nc.scalar.activation

            def x_high(b, k):
                act.wait_ge(x_in[k], 16 * (b + 1))
                go(x_hi[:, k, :], xt_raw[:, k, :], ACT.Copy).then_inc(x_hi_ready, 1)

            def mask_round(b):
                act.wait_ge(mask_in, 32 * (b + 1))
                go(mask_parts[0:S, :], mask_raw[0:S, :], ACT.Copy)
                go(mask_rnd[S:P, :], mask_raw[S:P, :], ACT.Copy).then_inc(mask_rounded, 1)

            def q_high(b, c, n):
                act.wait_ge(item_done, n + 1)
                for h in range(2):
                    r = slice(h * 64, h * 64 + 64)
                    go(q_parts[r, c % 2, h, :], ps_w[r, q_bank[c], :], ACT.Identity,
                       bias=bq_sb[r, c:c + 1]).then_inc(q_hi_done, 1)

            def other_blocks(b, c):
                for g in range(2):
                    act.wait_ge(max_done, 2 * (4 * b + c) + g + 1)
                    for h in range(2):
                        last = go(oth_max[64 * h:64 * h + 32, g, :], blk_max[64 * h + 32:64 * h + 64, g, :], ACT.Copy)
                    last.then_inc(oth_copied, 1)

            def exps(b, c):
                for g in range(2):
                    act.wait_ge(shifted, 2 * (4 * b + c) + g + 1)
                    go(probs[:, c % 2, 2 * g:2 * g + 2, :], ps_s[:, 2 * g:2 * g + 2, :], ACT.Exp).then_inc(exp_done, 1)

            def copy_out(b, c, again):
                act.wait_ge(pv_done, 4 * b + c + 1)
                if again:
                    act.wait_ge(norm_done, 4 * b - 4 + c + 1)
                go(o_raw[:, c, :], ps_o[:], ACT.Copy).then_inc(o_copied, 1)

            def o_high(bt, c):
                act.wait_ge(norm_done, 4 * bt + c + 1)
                go(o_hi[:, c, :], o_norm[:, c % 2, :], ACT.Copy).then_inc(o_hi_ready, 1)

            def scale(bt, t):
                act.wait_ge(gamma_done, 4 * bt + t + 1)
                act.wait_ge(rstd_done, 4 * bt + t + 1)
                go(y[:, t, :], y[:, t, :], ACT.Copy, scale=rstd[:, t:t + 1]).then_inc(scaled, 1)

            q_bank = {}

            def banks(tail):
                q_bank.update({1: bank_of("Q1", tail), 2: bank_of("Q2", tail), 3: bank_of("Q3", tail),
                               0: bank_of("Q0", tail)})

            act.wait_ge(k_in, 4 * 16)
            go(pick.rearrange("p (h o d) -> p h o d", h=KVH, d=HD),
               const[:, C_ID:C_ID + P].rearrange("p (h o d) -> p h o d", h=KVH, o=1).broadcast_to([P, KVH, P // HD, HD]),
               ACT.Copy)
            go(neg_pick[:], const[:, C_MAX:C_MAX + 2 * P], ACT.Copy)
            go(const_r[:], const[:, 0:C_ROUNDED], ACT.Copy).then_inc(const_rounded, 1)
            for part in range(2):
                act.wait_ge(rep_done, part + 1)
                go(k_rep[:, :, part, 0:4, :].rearrange("p b h s -> p h b s"),
                   ps_s[:, 0:2, :].rearrange("p k (e b s) -> p (k e) b s", e=2, b=B), ACT.Copy).then_inc(rep_copied_a, 1)
            for k in range(NC):
                x_high(0, k)
            mask_round(0)
            act.wait_ge(vec_in, 5 * 16)
            q_bank[0] = 0
            q_high(0, 0, 0)

            def batch(b, tail, nxt):
                banks(tail)
                other_blocks(b, 0)
                q_high(b, 1, item(b, "Q1", tail))
                exps(b, 0)
                if tail:
                    copy_out(b - 1, NC - 1, again=False)
                other_blocks(b, 1)
                q_high(b, 2, item(b, "Q2", tail))
                exps(b, 1)
                if not tail:
                    for k in range(NC):
                        act.wait_ge(res_in[k], 16)
                        go(wo_hi[:, k, :], res_x[:, k, :], ACT.Copy).then_inc(wo_hi_ready, 1)
                if tail:
                    o_high(b - 1, 0)
                copy_out(b, 0, again=tail)
                if tail:
                    for c in range(1, NC):
                        o_high(b - 1, c)
                other_blocks(b, 2)
                q_high(b, 3, item(b, "Q3", tail))
                exps(b, 2)
                copy_out(b, 1, again=tail)
                if nxt:
                    for k in range(NC):
                        x_high(b + 1, k)
                if tail:
                    scale(b - 1, 0)
                other_blocks(b, 3)
                if tail:
                    scale(b - 1, 1)
                exps(b, 3)
                copy_out(b, 2, again=tail)
                if nxt:
                    mask_round(b + 1)
                if nxt:
                    q_high(b + 1, 0, item(b, "Q0", tail))
                if tail:
                    scale(b - 1, 2)
                    scale(b - 1, 3)

            batch(0, tail=False, nxt=True)
            with act.Fori(1, B - 1) as b:
                batch(b, tail=True, nxt=True)
            batch(B - 1, tail=True, nxt=False)
            copy_out(B - 1, NC - 1, again=False)
            for c in range(NC):
                o_high(B - 1, c)
            for t in range(NC):
                scale(B - 1, t)

        @block.vector
        def _(dve):
            v = nc.vector

            def q_low(b, c, n, bank):
                for h in range(2):
                    r, o = slice(h * 64, h * 64 + 64), slice(64 - h * 64, 128 - h * 64)
                    dve.wait_ge(q_hi_done, 2 * (4 * b + c) + h + 1)
                    last = v.scalar_tensor_tensor(q_parts[o, c % 2, h, :], ps_w[r, bank, :], bq_sb[r, c:c + 1],
                                                  q_parts[r, c % 2, h, :].bitcast(F32), ALU.add, ALU.subtract)
                last.then_inc(q_read, 1)

            def maxima(b, c):
                for g in range(2):
                    G = 2 * (4 * b + c) + g
                    cols = max_cols[:, g, :, 0:6].rearrange("p n (j e) -> p j n e", e=3)
                    tok = tok_max[:, g, :].rearrange("p (j n) -> p j n", j=2)
                    rest = max_rest[:, g, :].rearrange("p (j n) -> p j n", j=2)
                    dve.wait_ge(scores_done, G + 1)
                    v.tensor_reduce(blk_max[:, g, :], ps_s[:, 2 * g:2 * g + 2, :].rearrange(
                        "p j (n r) -> p (j n) r", r=BLK), AX.X, ALU.max, apply_transpose=True).then_inc(max_done, 1)
                    dve.wait_ge(max_done, G + 1)
                    dve.wait_ge(oth_copied, G + 1)
                    v.tensor_tensor(tok_max[:, g, :], blk_max[:, g, :], oth_max[:, g, :], ALU.max).then_inc(tok_max_done, 1)
                    dve.wait_ge(tok_max_done, G + 1)
                    v.tensor_copy(cols[:, :, :, 0], tok).then_inc(max_top_done, 1)
                    dve.wait_ge(max_top_done, G + 1)
                    v.tensor_tensor(rest, tok, cols[:, :, :, 0], ALU.subtract).then_inc(max_rest_done, 1)
                    dve.wait_ge(max_rest_done, G + 1)
                    v.tensor_copy(cols[:, :, :, 1], rest).then_inc(max_mid_done, 1)
                    dve.wait_ge(max_mid_done, G + 1)
                    v.tensor_tensor(cols[:, :, :, 2], rest, cols[:, :, :, 1], ALU.subtract).then_inc(max_low_done, 1)
                    dve.wait_ge(max_low_done, G + 1)
                    v.transpose(max_rows[:, g, :], max_cols[:, g, :, :].rearrange("p n e -> p (n e)")).then_inc(max_ready, 1)

            def mask_low(b):
                dve.wait_ge(mask_rounded, b + 1)
                v.tensor_tensor(mask_parts[S:P, :], mask_raw[S:P, :], mask_rnd[S:P, :].bitcast(F32),
                                ALU.subtract).then_inc(mask_ready, 1)

            def reciprocals(b):
                dve.wait_ge(pv_done, 4 * b + 4)
                v.reciprocal(rsum[:], ps_z[:]).then_inc(z_read, 1)
                dve.wait_ge(z_read, b + 1)
                v.tensor_copy(rsum_hi[:], rsum[:]).then_inc(rsum_hi_done, 1)
                dve.wait_ge(rsum_hi_done, b + 1)
                v.tensor_tensor(rsum_lo[:], rsum[:], rsum_hi[:].bitcast(F32), ALU.subtract).then_inc(rsum_ready, 1)

            def normalise(bt, c, n, bank):
                dve.wait_ge(item_done, n + 1)
                dve.wait_ge(o_copied, 4 * bt + c + 1)
                if c >= 2:
                    dve.wait_ge(o_lo_ready, 4 * bt + c - 1)
                v.tensor_tensor(o_norm[:, c % 2, :], ps_w[:, bank, :], o_raw[:, c, :], ALU.mult).then_inc(norm_done, 1)

            def residual(bt, t, n, bank):
                dve.wait_ge(item_done, n + 1)
                dve.wait_ge(res_ready, 4 * bt + t + 1)
                dve.wait_ge(y_dma[t], 16 * (bt + 1))
                v.tensor_tensor(y[:, t, :], ps_w[:, bank, :], res_x[:, t, :], ALU.add).then_inc(resid_done, 1)

            def statistics(bt, t):
                dve.wait_ge(resid_done, 4 * bt + t + 1)
                v.bn_stats(stats[:, t, :], y[:, t, :]).then_inc(stats_done, 1)

            def mean_of(t):
                v.bn_aggr(mean_var[:, t, :], stats[:, t, :]).then_inc(mean_done, 1)

            def times_gamma(bt, t):
                dve.wait_ge(mean_done, 4 * bt + t + 1)
                v.scalar_tensor_tensor(y[:, t, :], y[:, t, :], mean_var[:, t, 0:1], gamma_sb[:],
                                       ALU.subtract, ALU.mult).then_inc(gamma_done, 1)

            def norm_pair(bt, t, n0, n1, between=None):
                residual(bt, t, *n0)
                statistics(bt, t)
                dve.wait_ge(stats_done, 4 * bt + t + 1)
                residual(bt, t + 1, *n1)
                mean_of(t)
                statistics(bt, t + 1)
                if between:
                    between()
                dve.wait_ge(stats_done, 4 * bt + t + 2)
                times_gamma(bt, t)
                mean_of(t + 1)
                times_gamma(bt, t + 1)

            dve.wait_ge(kt_done, 1)
            v.tensor_scalar(kt[:], ps_o[:, 0:B * S], bk_sb[:], SCALE, ALU.add, ALU.mult).then_inc(kt_added, 1)
            dve.wait_ge(kt_added, 1)
            v.tensor_copy(kt_hi[:], kt[:]).then_inc(kt_split, 1)
            dve.wait_ge(kt_split, 1)
            v.tensor_tensor(kt_lo[:], kt[:], kt_hi[:].bitcast(F32), ALU.subtract).then_inc(kt_split, 1)
            for part in range(2):
                dve.wait_ge(rep_done, part + 1)
                v.tensor_copy(k_rep[:, :, part, 4:8, :].rearrange("p b h s -> p h b s"),
                              ps_s[:, 2:4, :].rearrange("p k (e b s) -> p (k e) b s", e=2, b=B)).then_inc(rep_copied_d, 1)
            for k in range(NC):
                dve.wait_ge(y_dma[k], 16)
                v.tensor_copy(wq_hi[:, k, :], y[:, k, :]).then_inc(wq_hi_ready, 1)
                dve.wait_ge(wq_hi_ready, k + 1)
                v.tensor_tensor(wq_lo[:, k, :], y[:, k, :], wq_hi[:, k, :].bitcast(F32), ALU.subtract).then_inc(wq_lo_ready, 1)
                dve.wait_ge(x_hi_ready, k + 1)
                v.tensor_tensor(x_lo[:, k, :], xt_raw[:, k, :], x_hi[:, k, :].bitcast(F32), ALU.subtract).then_inc(x_lo_ready, 1)
            dve.wait_ge(v_done, 1)
            dve.wait_ge(vec_in, 5 * 16)
            v.tensor_tensor(v_rows[:], ps_z[:].rearrange("p (b n) -> p b n", b=B),
                            bv_sb[:].rearrange("p (o n) -> p o n", o=1).broadcast_to([P, B, P]), ALU.add).then_inc(v_copied, 1)
            dve.wait_ge(zeroed, 2)
            mask_low(0)
            q_low(0, 0, 0, 0)

            def batch(b, tail, nxt):
                def n(name):
                    return item(b, name, tail), bank_of(name, tail)
                maxima(b, 0)
                q_low(b, 1, *n("Q1"))
                if tail:
                    reciprocals(b - 1)
                maxima(b, 1)
                q_low(b, 2, *n("Q2"))
                if tail:
                    for c in range(NC):
                        normalise(b - 1, c, *n(f"R{c}"))
                maxima(b, 2)
                q_low(b, 3, *n("Q3"))
                if tail:
                    norm_pair(b - 1, 0, n("O0"), n("O1"))
                maxima(b, 3)
                if nxt:
                    mask_low(b + 1)
                if tail and nxt:
                    norm_pair(b - 1, 2, n("O2"), n("O3"), between=lambda: q_low(b + 1, 0, *n("Q0")))
                elif tail:
                    norm_pair(b - 1, 2, n("O2"), n("O3"))
                else:
                    q_low(b + 1, 0, *n("Q0"))

            batch(0, tail=False, nxt=True)
            with dve.Fori(1, B - 1) as b:
                batch(b, tail=True, nxt=True)
            batch(B - 1, tail=True, nxt=False)
            reciprocals(B - 1)
            for c in range(NC):
                normalise(B - 1, c, item(B, f"R{c}", True, True), bank_of(f"R{c}", True, True))
            for t in (0, 2):
                norm_pair(B - 1, t, *((item(B, f"O{u}", True, True), bank_of(f"O{u}", True, True)) for u in (t, t + 1)))

        @block.gpsimd
        def _(pool):
            gp = nc.gpsimd

            def k_blocks(b, c):
                kv = slice(KPC * c, KPC * (c + 1))
                head = const[:, C_HEAD:C_HEAD + GRP].rearrange("p (o g r) -> p o g r", o=1, r=1).broadcast_to([P, KPC, GRP, S])
                for part in range(2):
                    src = k_rep[:, b, part, kv, :] if isinstance(b, int) else \
                        k_rep[:, bass.ds(b, 1), part, kv, :].rearrange("p o h s -> p (o h) s")
                    last = gp.tensor_tensor(k_blk[:, part, kv, :, :],
                                            src.rearrange("p h (o s) -> p h o s", o=1).broadcast_to([P, KPC, GRP, S]),
                                            head, ALU.mult)
                last.then_inc(k_ready, 1)

            def v_blocks(b):
                src = v_rows[:, b, :] if isinstance(b, int) else v_rows[:, bass.ds(b, 1), :].rearrange("p o n -> p (o n)")
                half = const[:, C_HALF:C_HALF + 2].rearrange("p (o h r) -> p o h r", o=1, r=1).broadcast_to([P, KVH, 2, HD])
                gp.tensor_tensor(v_blk[:], src.rearrange("p (k o d) -> p k o d", k=KVH, o=1).broadcast_to([P, KVH, 2, HD]),
                                 half, ALU.mult).then_inc(v_ready, 1)

            def x_low(b, k):
                pool.wait_ge(x_hi_ready, 4 * b + k + 1)
                gp.tensor_tensor(x_lo[:, k, :], xt_raw[:, k, :], x_hi[:, k, :].bitcast(F32), ALU.subtract).then_inc(x_lo_ready, 1)

            def o_low(bt, c):
                pool.wait_ge(o_hi_ready, 4 * bt + c + 1)
                gp.tensor_tensor(o_lo[:, c, :], o_norm[:, c % 2, :], o_hi[:, c, :].bitcast(F32), ALU.subtract).then_inc(o_lo_ready, 1)

            def add_bo(bt, t):
                pool.wait_ge(res_in[t], 16 * (bt + 2))
                gp.tensor_tensor(res_x[:, t, :], res_x[:, t, :], bo_sb[:], ALU.add).then_inc(res_ready, 1)

            def inv_std(bt, t):
                m = 4 * bt + t + 1
                pool.wait_ge(mean_done, m)
                gp.tensor_tensor(var_eps[:, t:t + 1], mean_var[:, t, 1:2], eps[:], ALU.add).then_inc(eps_done, 1)
                pool.wait_ge(eps_done, m)
                gp.tensor_tensor(rstd[:, t:t + 1], var_eps[:, t:t + 1], neg_half[:], ALU.pow).then_inc(rstd_done, 1)

            def add_beta(bt, t):
                pool.wait_ge(scaled, 4 * bt + t + 1)
                gp.tensor_tensor(y[:, t, :], y[:, t, :], beta_sb[:], ALU.add).then_inc(y_ready, 1)

            gp.memset(max_cols[:], 0.0).then_inc(zeroed, 1)
            gp.memset(oth_max[:], 0.0).then_inc(zeroed, 1)
            gp.memset(eps[:], EPS).then_inc(zeroed, 1)
            gp.memset(neg_half[:], -0.5).then_inc(zeroed, 1)
            pool.wait_ge(rep_copied_a, 2)
            pool.wait_ge(rep_copied_d, 2)
            pool.wait_ge(k_in, 4 * 16)
            for c in range(NC):
                k_blocks(0, c)
            pool.wait_ge(v_copied, 1)
            pool.wait_ge(zeroed, 4)
            v_blocks(0)
            pool.wait_ge(vec_in, 5 * 16)

            def batch(b, tail, nxt):
                def blocks(c):
                    pool.wait_ge(scores_done, 2 * (4 * b + c) + 2)
                    k_blocks(b + 1, c)
                if nxt:
                    blocks(0)
                if tail:
                    for t in range(NC):
                        add_bo(b - 1, t)
                    pool.wait_ge(pv_done, 4 * b)
                    v_blocks(b)
                if nxt:
                    blocks(1)
                if tail:
                    for c in range(NC):
                        o_low(b - 1, c)
                else:
                    for k in range(NC):
                        pool.wait_ge(wo_hi_ready, k + 1)
                        gp.tensor_tensor(wo_lo[:, k, :], res_x[:, k, :], wo_hi[:, k, :].bitcast(F32),
                                         ALU.subtract).then_inc(wo_lo_ready, 1)
                if nxt:
                    blocks(2)
                    for k in range(NC):
                        x_low(b + 1, k)
                if tail:
                    inv_std(b - 1, 0)
                    inv_std(b - 1, 1)
                if nxt:
                    blocks(3)
                if tail:
                    add_beta(b - 1, 0)
                    add_beta(b - 1, 1)
                    inv_std(b - 1, 2)
                if tail:
                    add_beta(b - 1, 2)
                    inv_std(b - 1, 3)
                    add_beta(b - 1, 3)

            batch(0, tail=False, nxt=True)
            with pool.Fori(1, B - 1) as b:
                batch(b, tail=True, nxt=True)
            batch(B - 1, tail=True, nxt=False)
            for t in range(NC):
                add_bo(B - 1, t)
            for c in range(NC):
                o_low(B - 1, c)
            for t in range(NC):
                inv_std(B - 1, t)
                if t:
                    add_beta(B - 1, t - 1)
            add_beta(B - 1, NC - 1)


def constants():
    c = np.zeros((P, C_ALL), np.float32)
    r = np.arange(P)
    c[r, C_ID + r] = 1
    for j in range(2):
        for h in range(2):
            for part in range(3):
                c[64 * h + 3 * j + part, C_MAX + j * P + 64 * h:C_MAX + j * P + 64 * (h + 1)] = -1
    for part in range(2):
        for h in range(2):
            c[part * S + np.arange(S), C_MASK + h * S + np.arange(S)] = 1
    for chunk in range(NC):
        for pair in range(PAIRS):
            for h in range(2):
                row, col = BLK * pair + 2 * chunk + h, BLK * pair + HD * h
                c[row, C_SPREAD + chunk * P + col:C_SPREAD + chunk * P + col + HD] = 1
        for m in range(BLK):
            if m % 8 // 2 == chunk:
                c[S * (m % 2):S * (m % 2 + 1), C_SUM + chunk * BLK + m] = 1
    for g in range(GRP):
        c[:, C_HEAD + g] = (r % 64) // HD == g
    for h in range(2):
        c[:, C_HALF + h] = r // S == h
    return c


def kernel(x, ctx_2048, mask_Bx1xSxS2_ff0, L0_xattn_Wq, L0_xattn_bq, L0_xattn_Wk, L0_xattn_bk, L0_xattn_Wv,
           L0_xattn_bv, L0_xattn_Wo, L0_xattn_bo, L0_xattn_gamma, L0_xattn_beta):
    import concourse.bacc as bacc
    from concourse.bass_utils import run_bass_kernel_spmd

    x = np.asarray(x)
    arrays = {
        "x_t": x.transpose(0, 2, 1).reshape(B, NC, P, L),
        "x_n": x.reshape(B * L, D),
        "ctx_t": np.asarray(ctx_2048).reshape(B, S, NC, P).transpose(3, 2, 0, 1).reshape(P, NC, B * S),
        "mask_t": np.asarray(mask_Bx1xSxS2_ff0).reshape(B, L, S).transpose(0, 2, 1),
        "wq": np.asarray(L0_xattn_Wq),
        "bq": np.asarray(L0_xattn_bq).reshape(NC, P).T,
        "wk": np.asarray(L0_xattn_Wk),
        "bk": np.asarray(L0_xattn_bk).reshape(P, 1),
        "wv": np.asarray(L0_xattn_Wv),
        "bv": np.asarray(L0_xattn_bv),
        "wo": np.asarray(L0_xattn_Wo),
        "bo": np.asarray(L0_xattn_bo),
        "gamma": np.asarray(L0_xattn_gamma),
        "beta": np.asarray(L0_xattn_beta),
        "consts": constants(),
    }
    arrays = {name: np.ascontiguousarray(a) for name, a in arrays.items()}
    nc = bacc.Bacc("TRN2", target_bir_lowering=False, num_devices=1)
    args = {name: nc.dram_tensor(name, a.shape, mybir.dt.from_np(a.dtype), kind="ExternalInput").ap()
            for name, a in arrays.items()}
    out = nc.dram_tensor("out", (B * L, D), F32, kind="ExternalOutput").ap()
    cross_attention(nc, out=out, **args)
    result = run_bass_kernel_spmd(nc, [arrays], core_ids=[0])
    return result.results[0]["out"].reshape(B, L, D)
```

```python
from contextlib import ExitStack

import numpy as np

import concourse.bass as bass
from concourse import mybir

ALU = mybir.AluOpType
ACT = mybir.ActivationFunctionType
AX = mybir.AxisListType
F32 = mybir.dt.float32
F32R = mybir.dt.float32r
BF16 = mybir.dt.bfloat16

P = 128
B, L, S, D = 4, 512, 64, 512
NH, KVH = 32, 8
HD = D // NH
NC = D // P
HPC = NH // NC
KPC = KVH // NC
PAIRS = HPC // 2
GRP = NH // KVH
BLK = 32
NB = L // BLK
EPS = 1e-6
SCALE = 0.25

C_MASK, C_SPREAD = 0, P
C_ROUNDED = C_SPREAD + NC * P
C_ID, C_MAX = C_ROUNDED, C_ROUNDED + P
C_SUM = C_MAX + PAIRS * P
C_HEAD = C_SUM + (NC + 2) * BLK
C_HALF = C_HEAD + GRP
C_ALL = C_HALF + 2

ITEMS = {
    "lead": ["Q0", "Q1", "Q2"],
    "first": ["Q3", "Q0", "Q1", "Q2", "R0", "R1", "R2", "R3"],
    "loop": ["Q3", "O0", "O1", "Q0", "Q1", "O2", "Q2", "O3", "R0", "R1", "R2", "R3"],
    "last": ["Q3", "O0", "O1", "O2", "O3", "R0", "R1", "R2", "R3"],
}
BEFORE = len(ITEMS["lead"]) + len(ITEMS["first"])
PER_LOOP = len(ITEMS["loop"])


def item(b, name, part):
    at = ITEMS[part].index(name)
    if part == "lead":
        return at
    if part == "first":
        return len(ITEMS["lead"]) + at
    return PER_LOOP * b - PER_LOOP + BEFORE + at


def bank_of(name, part):
    return item(1, name, part) % 2


def cross_attention(nc, x_t, x_n, ctx_t, mask_t, wq, bq, wk, bk, wv, bv, wo, bo, gamma, beta, consts, out):
    with ExitStack() as ctx:
        def sb(name, shape, dt=F32):
            return ctx.enter_context(nc.sbuf_tensor(name, shape, dt))

        def sem(name):
            return ctx.enter_context(nc.semaphore(name))

        const = sb("const", [P, C_ALL])
        const_r = sb("const_r", [P, C_ROUNDED], F32R)
        ctx_sb = sb("ctx_sb", [P, NC, B * S])
        wk_sb = sb("wk_sb", [P, NC, P])
        wv_sb = sb("wv_sb", [P, NC, P])
        bq_sb = sb("bq_sb", [P, NC])
        bk_sb = sb("bk_sb", [P, 1])
        bv_sb = sb("bv_sb", [P, P])
        bo_sb = sb("bo_sb", [P, D])
        gamma_sb = sb("gamma_sb", [P, D])
        beta_sb = sb("beta_sb", [P, D])
        wq_hi = sb("wq_hi", [P, NC, D], F32R)
        wq_lo = sb("wq_lo", [P, NC, D], F32R)
        wo_hi = sb("wo_hi", [P, NC, D], F32R)
        wo_lo = sb("wo_lo", [P, NC, D], F32R)
        xt_raw = sb("xt_raw", [P, NC, L])
        x_hi = sb("x_hi", [P, NC, L], F32R)
        x_lo = sb("x_lo", [P, NC, L], F32R)
        kt = sb("kt", [P, B * S])
        kt_hi = sb("kt_hi", [P, B * S], F32R)
        kt_lo = sb("kt_lo", [P, B * S], F32R)
        k_rep = sb("k_rep", [P, B, 2, KVH, S])
        k_blk = sb("k_blk", [P, 2, KVH, GRP, S], F32R)
        v_rows = sb("v_rows", [P, B, P])
        v_blk = sb("v_blk", [P, KVH, 2, HD])
        mask_raw = sb("mask_raw", [P, L])
        mask_rnd = sb("mask_rnd", [P, L], F32R)
        mask_parts = sb("mask_parts", [P, L], F32R)
        q_parts = sb("q_parts", [P, 2, 2, L], F32R)
        blk_max = sb("blk_max", [P, PAIRS, NB])
        oth_max = sb("oth_max", [P, PAIRS, NB])
        tok_max = sb("tok_max", [P, PAIRS, NB])
        max_rest = sb("max_rest", [P, PAIRS, NB])
        max_cols = sb("max_cols", [P, NB, BLK], BF16)
        max_rows = sb("max_rows", [P, L], BF16)
        neg_pick = sb("neg_pick", [P, PAIRS * P], BF16)
        probs = sb("probs", [P, 2, PAIRS, L])
        o_sb = sb("o_sb", [P, NC, L])
        rsum = sb("rsum", [P, 2, L])
        rsum_hi = sb("rsum_hi", [P, 2, L], F32R)
        rsum_lo = sb("rsum_lo", [P, 2, L], F32R)
        o_hi = sb("o_hi", [P, NC, L], F32R)
        o_lo = sb("o_lo", [P, NC, L], F32R)
        res_x = sb("res_x", [P, NC, D])
        y = sb("y", [P, NC, D])
        stats = sb("stats", [P, NC, 6])
        mean_var = sb("mean_var", [P, NC, 2])
        var_eps = sb("var_eps", [P, NC])
        rstd = sb("rstd", [P, NC])
        eps = sb("eps", [P, 1])
        neg_half = sb("neg_half", [P, 1])

        ps_s = ctx.enter_context(nc.psum_tensor("ps_s", [P, PAIRS, L], F32))
        ps_o = ctx.enter_context(nc.psum_tensor("ps_o", [P, L], F32))
        ps_z = ctx.enter_context(nc.psum_tensor("ps_z", [P, L], F32))
        ps_w = ctx.enter_context(nc.psum_tensor("ps_w", [P, 2, L], F32))

        k_in = sem("k_in")
        const_in = sem("const_in")
        bk_in = sem("bk_in")
        bq_in = sem("bq_in")
        v_in = sem("v_in")
        vec_in = sem("vec_in")
        y_dma = [sem(f"y_dma{t}") for t in range(NC)]
        res_in = [sem(f"res_in{t}") for t in range(NC)]
        last_x_in = [sem(f"last_x_in{t}") for t in range(NC)]
        x_in = [sem(f"x_in{k}") for k in range(NC)]
        mask_in = sem("mask_in")
        zeroed = sem("zeroed")
        pick_ready = sem("pick_ready")
        const_rounded = sem("const_rounded")
        neg_pick_ready = sem("neg_pick_ready")
        kt_done = sem("kt_done")
        kt_added = sem("kt_added")
        kt_split = sem("kt_split")
        rep_done = sem("rep_done")
        rep_copied_a = sem("rep_copied_a")
        rep_copied_d = sem("rep_copied_d")
        v_done = sem("v_done")
        v_copied = sem("v_copied")
        wq_hi_ready = sem("wq_hi_ready")
        wq_lo_ready = sem("wq_lo_ready")
        wo_hi_ready = sem("wo_hi_ready")
        wo_lo_ready = sem("wo_lo_ready")
        x_hi_ready = sem("x_hi_ready")
        x_lo_ready = sem("x_lo_ready")
        k_ready = sem("k_ready")
        v_ready = sem("v_ready")
        mask_rounded = sem("mask_rounded")
        mask_ready = sem("mask_ready")
        scores_done = sem("scores_done")
        max_done = sem("max_done")
        oth_copied = sem("oth_copied")
        max_top_done = sem("max_top_done")
        max_mid_done = sem("max_mid_done")
        max_low_done = sem("max_low_done")
        max_ready = sem("max_ready")
        shifted = sem("shifted")
        exp_done = sem("exp_done")
        pv_done = sem("pv_done")
        o_copied = sem("o_copied")
        z_read = sem("z_read")
        rsum_hi_done = sem("rsum_hi_done")
        rsum_ready = sem("rsum_ready")
        item_done = sem("item_done")
        last_out_done = sem("last_out_done")
        q_read = sem("q_read")
        q_hi_done = sem("q_hi_done")
        norm_done = sem("norm_done")
        o_hi_ready = sem("o_hi_ready")
        o_lo_ready = sem("o_lo_ready")
        end_lo_ready = sem("end_lo_ready")
        res_ready = sem("res_ready")
        resid_done = sem("resid_done")
        stats_done = sem("stats_done")
        mean_done = sem("mean_done")
        gamma_done = sem("gamma_done")
        eps_done = sem("eps_done")
        rstd_done = sem("rstd_done")
        scaled = sem("scaled")
        y_ready = sem("y_ready")
        end_y_ready = sem("end_y_ready")

        pick = o_hi[:, 0:KVH * P // L, :].rearrange("p c n -> p (c n)")

        block = ctx.enter_context(nc.Block())

        def row(a):
            return a.rearrange("(o n) -> o n", o=1)

        @block.sync
        def _(sp):
            sp.dma_start(ctx_sb[:], ctx_t).then_inc(k_in, 16)
            sp.dma_start(const[:], consts).then_inc(const_in, 16)
            sp.dma_start(bk_sb[:], bk).then_inc(bk_in, 16)
            for k in range(NC):
                sp.dma_start(xt_raw[:, k, :], x_t[0, k]).then_inc(x_in[k], 16)
            sp.dma_start(bq_sb[:], bq).then_inc(bq_in, 16)
            for h in range(2):
                sp.dma_start(mask_raw[h * S:(h + 1) * S, :], mask_t[0]).then_inc(mask_in, 16)
            sp.dma_start(wv_sb[:], wv.rearrange("(k p) n -> p k n", p=P)).then_inc(v_in, 16)
            sp.dma_start(bv_sb[:], row(bv).broadcast_to([P, P])).then_inc(v_in, 16)
            sp.dma_start(bo_sb[:], row(bo).broadcast_to([P, D])).then_inc(vec_in, 16)
            sp.dma_start(gamma_sb[:], row(gamma).broadcast_to([P, D])).then_inc(vec_in, 16)
            sp.dma_start(beta_sb[:], row(beta).broadcast_to([P, D])).then_inc(vec_in, 16)
            for t in range(NC):
                sp.dma_start(res_x[:, t, :], wo[t * P:(t + 1) * P, :]).then_inc(res_in[t], 16)

            def store(bt, t):
                sp.wait_ge(y_ready, 4 * bt + t + 1)
                sp.dma_start(out[bass.ds((bt * NC + t) * P, P), :], y[:, t, :]).then_inc(y_dma[t], 16)

            def load_next(b):
                sp.wait_ge(x_lo_ready, 4 * b + 4)
                for k in range(NC):
                    sp.dma_start(xt_raw[:, k, :], x_t[b + 1, k] if isinstance(b, int) else
                                 x_t[bass.ds(b + 1, 1), k].rearrange("o p n -> (o p) n")).then_inc(x_in[k], 16)
                sp.wait_ge(mask_ready, b + 1)
                for h in range(2):
                    sp.dma_start(mask_raw[h * S:(h + 1) * S, :], mask_t[b + 1] if isinstance(b, int) else
                                 mask_t[bass.ds(b + 1, 1)].rearrange("o p n -> (o p) n")).then_inc(mask_in, 16)

            def tails(b, part):
                if part == "last":
                    sp.wait_ge(x_lo_ready, 4 * b + 4)
                for t in range(NC):
                    if part == "first":
                        sp.wait_ge(wo_lo_ready, t + 1)
                    elif part == "loop":
                        sp.wait_ge(resid_done, 4 * b - 4 + t + 1)
                    place, loaded = (xt_raw, last_x_in) if part == "last" else (res_x, res_in)
                    sp.dma_start(place[:, t, :], x_n[bass.ds((b * NC + t) * P, P), :]).then_inc(loaded[t], 16)
                    if part == "loop":
                        store(b - 1, t)
                if part == "last":
                    for t in range(NC):
                        store(b - 1, t)

            load_next(0)
            tails(0, "first")
            with sp.Fori(1, B - 1) as b:
                load_next(b)
                tails(b, "loop")
            tails(B - 1, "last")
            for t in range(2):
                store(B - 1, t)
            for t in range(2, NC):
                sp.wait_ge(end_y_ready, t - 1)
                sp.dma_start(out[((B - 1) * NC + t) * P:((B - 1) * NC + t + 1) * P, :], y[:, t, :]).then_inc(y_dma[t], 16)
            for t in range(NC):
                sp.wait_ge(y_dma[t], 16 * (B + 1))

        @block.tensor
        def _(pe):
            mm = nc.tensor.matmul

            def q_item(b, c, bank, free=None, halfway=None):
                dst = ps_w[:, bank, :]
                if free:
                    pe.wait_ge(*free)
                for k in range(NC):
                    if halfway and k == 2:
                        halfway()
                    if c == 0:
                        if isinstance(b, int) and b == 0:
                            pe.wait_ge(wq_lo_ready, k + 1)
                        pe.wait_ge(x_lo_ready, 4 * b + k + 1)
                    wh = wq_hi[:, k, c * P:(c + 1) * P]
                    wl = wq_lo[:, k, c * P:(c + 1) * P]
                    mm(dst, wh, x_hi[:, k, :], start=k == 0, stop=False)
                    mm(dst, wh, x_lo[:, k, :], start=False, stop=False)
                    last = mm(dst, wl, x_hi[:, k, :], start=False, stop=k == NC - 1)
                last.then_inc(item_done, 1)

            def spread_item(bt, c, bank, free=None, second=0):
                pe.wait_ge(rsum_ready, bt + 1 + second)
                if free:
                    pe.wait_ge(*free)
                sel = const_r[:, C_SPREAD + c * P:C_SPREAD + (c + 1) * P]
                mm(ps_w[:, bank, :], sel, rsum_hi[:, second, :], start=True, stop=False)
                mm(ps_w[:, bank, :], sel, rsum_lo[:, second, :], start=False, stop=True).then_inc(item_done, 1)

            def out_products(dst, c, t, first=True):
                oh = o_hi[:, c, t * P:(t + 1) * P]
                ol = o_lo[:, c, t * P:(t + 1) * P]
                mm(dst, oh, wo_hi[:, c, :], start=first and c == 0, stop=False, skip_group_check=True)
                mm(dst, oh, wo_lo[:, c, :], start=False, stop=False, skip_group_check=True)
                return mm(dst, ol, wo_hi[:, c, :], start=False, stop=c == NC - 1, skip_group_check=True)

            def out_item(bt, t, bank, free=None):
                if free:
                    pe.wait_ge(*free)
                pe.wait_ge(o_lo_ready, 4 * bt + 4)
                for c in range(NC):
                    last = out_products(ps_w[:, bank, :], c, t)
                last.then_inc(item_done, 1)

            def scores(b, c):
                i = 4 * b + c
                pe.wait_ge(q_read, i + 1)
                pe.wait_ge(k_ready, i + 1)
                if c == 0:
                    pe.wait_ge(mask_ready, b + 1)
                for j in range(PAIRS):
                    if j % 2 == 0 and not (isinstance(i, int) and i == 0):
                        pe.wait_ge(exp_done, 2 * i - 1 + j // 2)
                    kv, g = KPC * c + j // 2, 2 * (j % 2)
                    q = q_parts[:, c % 2, j // 2, :]
                    mm(ps_s[:, j, :], k_blk[:, 0, kv, g:g + 2, :], q, start=True, stop=False, skip_group_check=True)
                    mm(ps_s[:, j, :], k_blk[:, 1, kv, g:g + 2, :], q, start=False, stop=False, skip_group_check=True)
                    last = mm(ps_s[:, j, :], const_r[:, C_MASK:C_MASK + P], mask_parts[:],
                              start=False, stop=True, skip_group_check=True)
                    if j % 2 == 1:
                        last.then_inc(scores_done, 1)

            def shift(b, c):
                if isinstance(b, int) and b == 0 and c == 0:
                    pe.wait_ge(neg_pick_ready, 1)
                pe.wait_ge(max_ready, 4 * b + c + 1)
                for j in range(PAIRS):
                    last = mm(ps_s[:, j, :], neg_pick[:, j * P:(j + 1) * P], max_rows[:],
                              start=False, stop=True, skip_group_check=True)
                    if j % 2 == 1:
                        last.then_inc(shifted, 1)

            def outputs(b, c):
                i = 4 * b + c
                pe.wait_ge(exp_done, 2 * i + 2)
                if not (isinstance(i, int) and i == 0):
                    pe.wait_ge(o_copied, i)
                if c == 0:
                    pe.wait_ge(v_ready, b + 1)
                for j in range(PAIRS):
                    mm(ps_o[BLK * j:BLK * (j + 1), :], v_blk[:, KPC * c + j // 2, :, :], probs[:, c % 2, j, :],
                       start=True, stop=True)

            def sums(b, c, split=False):
                if c == 0 and isinstance(b, int) and b == 0:
                    pe.wait_ge(v_copied, 2)
                elif c == 0:
                    pe.wait_ge(z_read, b)
                if split and c == 3:
                    pe.wait_ge(z_read, b + 1)
                rows = c + 2 if split and c >= 2 else c
                for j in range(PAIRS):
                    last = mm(ps_z[BLK * j:BLK * (j + 1), :], const[:, C_SUM + rows * BLK:C_SUM + (rows + 1) * BLK],
                              probs[:, c % 2, j, :], start=c == 0 or split and c == 3,
                              stop=c == NC - 1 or split and c == 2, skip_group_check=True)
                last.then_inc(pv_done, 1)

            def shift_with_values(b, c, before, split=False):
                last_step = (b, c - 1) if c else (b - 1, NC - 1)
                if before:
                    outputs(*last_step)
                shift(b, c)
                if not before:
                    outputs(*last_step)
                sums(*last_step, split)

            pe.wait_ge(k_in, 2 * 16)
            for k in range(NC):
                last = mm(ps_o[:, 0:B * S], wk_sb[:, k, :], ctx_sb[:, k, :], start=k == 0, stop=k == NC - 1)
            last.then_inc(kt_done, 1)

            def v_item(half):
                if half == 0:
                    pe.wait_ge(v_in, 2 * 16)
                else:
                    pe.wait_ge(v_copied, 1)
                for b in (2 * half, 2 * half + 1):
                    for k in range(NC):
                        for h in range(2):
                            last = mm(ps_z[h * S:(h + 1) * S, b * P:(b + 1) * P], ctx_sb[:, k, b * S:(b + 1) * S],
                                      wv_sb[:, k, :], start=k == 0, stop=k == NC - 1)
                last.then_inc(v_done, 1)

            def replicate(half):
                for part, parts in enumerate((kt_hi, kt_lo)):
                    if half == 0:
                        pe.wait_ge(kt_split, part + 1)
                    elif part:
                        pe.wait_ge(rep_copied_d, 1)
                    else:
                        pe.wait_ge(rep_copied_a, 1)
                    for i in range(KVH // 2):
                        kv = half * KVH // 2 + i
                        last = mm(ps_s[:, 2 * part + i // 2, (i % 2) * B * S:(i % 2 + 1) * B * S],
                                  pick[:, kv * P:(kv + 1) * P], parts[:], start=True, stop=True)
                last.then_inc(rep_done, 1)

            pe.wait_ge(pick_ready, 1)
            replicate(0)
            q_item(0, 0, bank_of("Q0", "lead"), halfway=lambda: replicate(1))
            pe.wait_ge(const_rounded, 1)
            pe.wait_ge(rep_copied_a, 2)
            pe.wait_ge(rep_copied_d, 2)

            def pair_of_steps(b, part):
                tail = part == "loop"
                scores(b + 1, 0)
                q_item(b + 1, 1, bank_of("Q1", part), (resid_done, 4 * b - 2) if tail else None)
                if tail:
                    out_item(b - 1, 2, bank_of("O2", part))
                elif part == "lead":
                    v_item(0)
                if part == "lead":
                    shift(b + 1, 0)
                else:
                    shift_with_values(b + 1, 0, before=not tail)
                scores(b + 1, 1)
                q_item(b + 1, 2, bank_of("Q2", part))
                if tail:
                    out_item(b - 1, 3, bank_of("O3", part), (resid_done, 4 * b - 1))
                elif part == "lead":
                    v_item(1)
                if not tail:
                    shift_with_values(b + 1, 1, before=True)
                else:
                    shift(b + 1, 1)
                if part == "loop":
                    spread_item(b, 0, bank_of("R0", part), (q_read, 4 * b + 7))
                    spread_item(b, 1, bank_of("R1", part), (resid_done, 4 * b))
                    outputs(b + 1, 0)
                    sums(b + 1, 0)
                elif part == "first":
                    spread_item(b, 0, bank_of("R0", part))
                    spread_item(b, 1, bank_of("R1", part), (q_read, 4 * b + 7))
                if part != "lead":
                    spread_item(b, 2, bank_of("R2", part), (norm_done, 4 * b + 1))
                    spread_item(b, 3, bank_of("R3", part), (norm_done, 4 * b + 2))

            def iteration(b, part):
                tail = part != "first"
                scores(b, 2)
                q_item(b, 3, bank_of("Q3", part), (norm_done, 4 * b - 1) if tail else None)
                if tail:
                    out_item(b - 1, 0, bank_of("O0", part))
                shift_with_values(b, 2, before=not tail)
                scores(b, 3)
                if tail:
                    out_item(b - 1, 1, bank_of("O1", part))
                if part != "last":
                    q_item(b + 1, 0, bank_of("Q0", part), (resid_done, 4 * b - 3) if tail else None)
                else:
                    out_item(b - 1, 2, bank_of("O2", part), (resid_done, 4 * b - 3))
                shift_with_values(b, 3, before=not tail, split=part == "last")
                if part == "last":
                    out_item(b - 1, 3, bank_of("O3", part), (resid_done, 4 * b - 2))
                else:
                    pair_of_steps(b, part)

            pair_of_steps(-1, "lead")
            iteration(0, "first")
            pe.wait_ge(wo_lo_ready, NC)
            with pe.Fori(1, B - 1) as b:
                iteration(b, "loop")
            iteration(B - 1, "last")
            b = B - 1

            def start_tile(t):
                pe.wait_ge(res_ready, 4 * b + t + 1)
                mm(ps_s[:, t, :], const[:, C_ID:C_ID + P], xt_raw[:, t, :], start=True, stop=False, skip_group_check=True)

            pe.wait_ge(exp_done, 8 * B)
            start_tile(0)
            outputs(b, 3)
            sums(b, 3, split=True)
            spread_item(b, 0, bank_of("R0", "last"), (resid_done, 4 * b - 1))
            spread_item(b, 1, bank_of("R1", "last"), (resid_done, 4 * b))
            start_tile(1)
            spread_item(b, 2, bank_of("R2", "last"), (norm_done, 4 * b + 1))
            start_tile(2)
            start_tile(3)
            for c in range(NC):
                if c in (0, 3):
                    pe.wait_ge(end_lo_ready, 1 + c // 3)
                else:
                    pe.wait_ge(o_lo_ready, 4 * b + c)
                for t in range(NC):
                    last = out_products(ps_s[:, t, :], c, t, first=False)
                    if c == 3:
                        last.then_inc(last_out_done, 1)
                    if c == 2 and t == 0:
                        spread_item(b, 3, bank_of("R3", "last"), (norm_done, 4 * b + 2), second=1)

        @block.scalar
        def _(act):
            act.dma_start(wk_sb[:], wk.rearrange("(k p) n -> p k n", p=P)).then_inc(k_in, 16)
            for k in range(NC):
                act.dma_start(y[:, k, :], wq[k * P:(k + 1) * P, :]).then_inc(y_dma[k], 16)
            go = nc.scalar.activation

            def x_high(b, k):
                act.wait_ge(x_in[k], 16 * (b + 1))
                go(x_hi[:, k, :], xt_raw[:, k, :], ACT.Copy).then_inc(x_hi_ready, 1)

            def mask_round(b):
                act.wait_ge(mask_in, 32 * (b + 1))
                go(mask_parts[0:S, :], mask_raw[0:S, :], ACT.Copy)
                go(mask_rnd[S:P, :], mask_raw[S:P, :], ACT.Copy).then_inc(mask_rounded, 1)

            def q_high(b, c, n, bank):
                act.wait_ge(item_done, n + 1)
                for h in range(2):
                    r = slice(h * 64, h * 64 + 64)
                    go(q_parts[r, c % 2, h, :], ps_w[r, bank, :], ACT.Identity,
                       bias=bq_sb[r, c:c + 1]).then_inc(q_hi_done, 1)

            def exps(b, c):
                for g in range(2):
                    act.wait_ge(shifted, 2 * (4 * b + c) + g + 1)
                    go(probs[:, c % 2, 2 * g:2 * g + 2, :], ps_s[:, 2 * g:2 * g + 2, :], ACT.Exp).then_inc(exp_done, 1)

            def copy_out(b, c, again):
                act.wait_ge(pv_done, 4 * b + c + 1)
                if again:
                    act.wait_ge(o_lo_ready, 4 * b - 4 + c + 1)
                go(o_sb[:, c, :], ps_o[:], ACT.Copy).then_inc(o_copied, 1)

            def rsum_high(b):
                act.wait_ge(z_read, b + 1)
                go(rsum_hi[:, 0, :], rsum[:, 0, :], ACT.Copy).then_inc(rsum_hi_done, 1)

            def o_high(bt, c):
                act.wait_ge(norm_done, 4 * bt + c + 1)
                go(o_hi[:, c, :], o_sb[:, c, :], ACT.Copy).then_inc(o_hi_ready, 1)

            def scale(bt, t):
                act.wait_ge(gamma_done, 4 * bt + t + 1)
                act.wait_ge(rstd_done, 4 * bt + t + 1)
                go(y[:, t, :], y[:, t, :], ACT.Copy, scale=rstd[:, t:t + 1]).then_inc(scaled, 1)

            act.wait_ge(zeroed, 4)
            go(var_eps[:, 0:1], eps[:], ACT.Exp)
            act.wait_ge(const_in, 16)
            go(pick.rearrange("p (h o d) -> p h o d", h=KVH, d=HD),
               const[:, C_ID:C_ID + P].rearrange("p (h o d) -> p h o d", h=KVH, o=1).broadcast_to([P, KVH, P // HD, HD]),
               ACT.Copy).then_inc(pick_ready, 1)
            for k in range(NC):
                x_high(0, k)

            def copy_hi(half):
                act.wait_ge(rep_done, half + 1)
                kv = slice(half * KVH // 2, (half + 1) * KVH // 2)
                go(k_rep[:, :, 0, kv, :].rearrange("p b h s -> p h b s"),
                   ps_s[:, 0:2, :].rearrange("p k (e b s) -> p (k e) b s", e=2, b=B), ACT.Copy).then_inc(rep_copied_a, 1)

            copy_hi(0)
            go(const_r[:], const[:, 0:C_ROUNDED], ACT.Copy).then_inc(const_rounded, 1)
            copy_hi(1)
            mask_round(0)
            act.wait_ge(bq_in, 16)
            q_high(0, 0, item(0, "Q0", "lead"), bank_of("Q0", "lead"))
            go(neg_pick[:], const[:, C_MAX:C_MAX + PAIRS * P], ACT.Copy).then_inc(neg_pick_ready, 1)

            def pair_of_steps(b, part):
                tail = part == "loop"
                q_high(b + 1, 1, item(b, "Q1", part), bank_of("Q1", part))
                exps(b + 1, 0)
                if part != "lead":
                    copy_out(b, 3, again=tail)
                if tail:
                    scale(b - 1, 1)
                if part != "lead":
                    rsum_high(b)
                q_high(b + 1, 2, item(b, "Q2", part), bank_of("Q2", part))
                exps(b + 1, 1)
                if part != "lead":
                    o_high(b, 0)
                    o_high(b, 1)
                copy_out(b + 1, 0, again=part != "lead")
                if tail:
                    scale(b - 1, 2)
                if part != "lead":
                    o_high(b, 2)
                    o_high(b, 3)
                if tail:
                    scale(b - 1, 3)

            def iteration(b, part):
                tail = part != "first"
                q_high(b, 3, item(b, "Q3", part), bank_of("Q3", part))
                exps(b, 2)
                copy_out(b, 1, again=tail)
                if part != "last":
                    for k in range(NC):
                        x_high(b + 1, k)
                    act.wait_ge(scores_done, 8 * b + 8)
                    mask_round(b + 1)
                    q_high(b + 1, 0, item(b, "Q0", part), bank_of("Q0", part))
                exps(b, 3)
                copy_out(b, 2, again=tail)
                if tail:
                    scale(b - 1, 0)
                if part == "first":
                    for k in range(NC):
                        act.wait_ge(res_in[k], 16)
                        go(wo_hi[:, k, :], res_x[:, k, :], ACT.Copy).then_inc(wo_hi_ready, 1)
                if part != "last":
                    pair_of_steps(b, part)

            pair_of_steps(-1, "lead")
            iteration(0, "first")
            with act.Fori(1, B - 1) as b:
                iteration(b, "loop")
            iteration(B - 1, "last")
            copy_out(B - 1, 3, again=True)
            for c in range(3):
                o_high(B - 1, c)
            scale(B - 2, 1)
            o_high(B - 1, 3)
            scale(B - 2, 2)
            scale(B - 2, 3)
            for t in range(NC):
                scale(B - 1, t)

        @block.vector
        def _(dve):
            v = nc.vector

            def q_low(b, c, bank):
                for h in range(2):
                    r, o = slice(h * 64, h * 64 + 64), slice(64 - h * 64, 128 - h * 64)
                    dve.wait_ge(q_hi_done, 2 * (4 * b + c) + h + 1)
                    last = v.scalar_tensor_tensor(q_parts[o, c % 2, h, :], ps_w[r, bank, :], bq_sb[r, c:c + 1],
                                                  q_parts[r, c % 2, h, :].bitcast(F32), ALU.add, ALU.subtract)
                last.then_inc(q_read, 1)

            def maxima(b, c, tile=None):
                i = 4 * b + c
                cols = max_cols[:, :, 0:3 * PAIRS].rearrange("p n (j e) -> p j n e", e=3)
                for g in range(2):
                    dve.wait_ge(scores_done, 2 * i + g + 1)
                    if tile and g == 0:
                        dve.wait_ge(stats_done, 4 * tile[0] + tile[1] + 1)
                    v.tensor_reduce(blk_max[:, 2 * g:2 * g + 2, :], ps_s[:, 2 * g:2 * g + 2, :].rearrange(
                        "p j (n r) -> p j n r", r=BLK), AX.X, ALU.max, apply_transpose=True).then_inc(max_done, 1)
                    if tile and g == 0:
                        mean_of(tile[1])
                dve.wait_ge(max_done, 2 * i + 2)
                for h in range(2):
                    last = v.tensor_copy(oth_max[64 * h:64 * h + 32, :, :], blk_max[64 * h + 32:64 * h + 64, :, :])
                last.then_inc(oth_copied, 1)
                dve.wait_ge(oth_copied, i + 1)
                v.tensor_tensor(tok_max[:], blk_max[:], oth_max[:], ALU.max)
                v.tensor_tensor(cols[:, :, :, 0], blk_max[:], oth_max[:], ALU.max).then_inc(max_top_done, 1)
                dve.wait_ge(max_top_done, i + 1)
                v.tensor_tensor(max_rest[:], tok_max[:], cols[:, :, :, 0], ALU.subtract)
                v.tensor_tensor(cols[:, :, :, 1], tok_max[:], cols[:, :, :, 0], ALU.subtract).then_inc(max_mid_done, 1)
                dve.wait_ge(max_mid_done, i + 1)
                v.tensor_tensor(cols[:, :, :, 2], max_rest[:], cols[:, :, :, 1], ALU.subtract).then_inc(max_low_done, 1)
                dve.wait_ge(max_low_done, i + 1)
                v.transpose(max_rows[:], max_cols[:].rearrange("p n e -> p (n e)")).then_inc(max_ready, 1)

            def mask_low(b):
                dve.wait_ge(mask_rounded, b + 1)
                v.tensor_tensor(mask_parts[S:P, :], mask_raw[S:P, :], mask_rnd[S:P, :].bitcast(F32),
                                ALU.subtract).then_inc(mask_ready, 1)

            def reciprocals(b, tile=None, chunks=NC, second=0):
                dve.wait_ge(pv_done, 4 * b + chunks)
                if tile:
                    dve.wait_ge(stats_done, 4 * tile[0] + tile[1] + 1)
                v.reciprocal(rsum[:, second, :], ps_z[:]).then_inc(z_read, 1)
                if tile:
                    mean_of(tile[1])

            def split_reciprocals(b, second):
                dve.wait_ge(z_read, b + 1 + second)
                v.tensor_copy(rsum_hi[:, second, :], rsum[:, second, :]).then_inc(rsum_hi_done, 1)
                dve.wait_ge(rsum_hi_done, b + 1 + second)
                v.tensor_tensor(rsum_lo[:, second, :], rsum[:, second, :], rsum_hi[:, second, :].bitcast(F32),
                                ALU.subtract).then_inc(rsum_ready, 1)

            def end_low(b, c):
                dve.wait_ge(o_hi_ready, 4 * b + c + 1)
                v.tensor_tensor(o_lo[:, c, :], o_sb[:, c, :], o_hi[:, c, :].bitcast(F32), ALU.subtract).then_inc(end_lo_ready, 1)

            def normalise(b, c, part, tile=None):
                dve.wait_ge(item_done, item(b, f"R{c}", part) + 1)
                dve.wait_ge(o_copied, 4 * b + c + 1)
                if tile:
                    dve.wait_ge(stats_done, 4 * tile[0] + tile[1] + 1)
                v.tensor_tensor(o_sb[:, c, :], ps_w[:, bank_of(f"R{c}", part), :], o_sb[:, c, :],
                                ALU.mult).then_inc(norm_done, 1)
                if tile:
                    mean_of(tile[1])

            def residual(bt, t, part, tile=None):
                dve.wait_ge(item_done, item(bt + 1, f"O{t}", part) + 1)
                dve.wait_ge(res_ready, 4 * bt + t + 1)
                dve.wait_ge(y_dma[t], 16 * (bt + 1))
                if tile:
                    dve.wait_ge(stats_done, 4 * tile[0] + tile[1] + 1)
                v.tensor_tensor(y[:, t, :], ps_w[:, bank_of(f"O{t}", part), :], res_x[:, t, :], ALU.add).then_inc(resid_done, 1)
                if tile:
                    mean_of(tile[1])

            def statistics(bt, t):
                dve.wait_ge(resid_done, 4 * bt + t + 1)
                v.bn_stats(stats[:, t, :], y[:, t, :]).then_inc(stats_done, 1)

            def mean_of(t):
                v.bn_aggr(mean_var[:, t, :], stats[:, t, :]).then_inc(mean_done, 1)

            def times_gamma(bt, t, src=y):
                dve.wait_ge(mean_done, 4 * bt + t + 1)
                if src is not y:
                    dve.wait_ge(y_dma[t], 16 * (bt + 1))
                v.scalar_tensor_tensor(y[:, t, :], src[:, t, :], mean_var[:, t, 0:1], gamma_sb[:],
                                       ALU.subtract, ALU.mult).then_inc(gamma_done, 1)

            def wq_split(k):
                dve.wait_ge(y_dma[k], 16)
                v.tensor_copy(wq_hi[:, k, :], y[:, k, :]).then_inc(wq_hi_ready, 1)
                dve.wait_ge(wq_hi_ready, k + 1)
                v.tensor_tensor(wq_lo[:, k, :], y[:, k, :], wq_hi[:, k, :].bitcast(F32), ALU.subtract).then_inc(wq_lo_ready, 1)

            def copy_lo(half):
                dve.wait_ge(rep_done, half + 1)
                kv = slice(half * KVH // 2, (half + 1) * KVH // 2)
                v.tensor_copy(k_rep[:, :, 1, kv, :].rearrange("p b h s -> p h b s"),
                              ps_s[:, 2:4, :].rearrange("p k (e b s) -> p (k e) b s", e=2, b=B)).then_inc(rep_copied_d, 1)

            def v_copy(half):
                dve.wait_ge(v_done, half + 1)
                b = slice(2 * half, 2 * half + 2)
                v.tensor_tensor(v_rows[:, b, :], ps_z[:].rearrange("p (b n) -> p b n", b=B)[:, b, :],
                                bv_sb[:].rearrange("p (o n) -> p o n", o=1).broadcast_to([P, 2, P]), ALU.add).then_inc(v_copied, 1)

            wq_split(0)
            wq_split(1)
            dve.wait_ge(bk_in, 16)
            dve.wait_ge(kt_done, 1)
            v.tensor_scalar(kt[:], ps_o[:, 0:B * S], bk_sb[:], SCALE, ALU.add, ALU.mult).then_inc(kt_added, 1)
            dve.wait_ge(kt_added, 1)
            v.tensor_copy(kt_hi[:], kt[:]).then_inc(kt_split, 1)
            dve.wait_ge(kt_split, 1)
            v.tensor_tensor(kt_lo[:], kt[:], kt_hi[:].bitcast(F32), ALU.subtract).then_inc(kt_split, 1)
            wq_split(2)
            copy_lo(0)
            wq_split(3)
            copy_lo(1)
            dve.wait_ge(zeroed, 2)
            mask_low(0)
            q_low(0, 0, bank_of("Q0", "lead"))

            def pair_of_steps(b, part):
                tail = part == "loop"
                maxima(b + 1, 0, (b - 1, 1) if tail else None)
                q_low(b + 1, 1, bank_of("Q1", part))
                if part == "lead":
                    dve.wait_ge(v_in, 2 * 16)
                    v_copy(0)
                if tail:
                    times_gamma(b - 1, 1)
                    residual(b - 1, 2, part)
                    statistics(b - 1, 2)
                if part != "lead":
                    reciprocals(b, (b - 1, 2) if tail else None)
                maxima(b + 1, 1)
                q_low(b + 1, 2, bank_of("Q2", part))
                if part == "lead":
                    v_copy(1)
                if tail:
                    residual(b - 1, 3, part)
                    times_gamma(b - 1, 2)
                    statistics(b - 1, 3)
                if part != "lead":
                    normalise(b, 0, part, (b - 1, 3) if tail else None)
                    normalise(b, 1, part)
                    if tail:
                        times_gamma(b - 1, 3)
                    normalise(b, 2, part)
                    normalise(b, 3, part)

            def iteration(b, part):
                tail = part != "first"
                maxima(b, 2)
                q_low(b, 3, bank_of("Q3", part))
                if tail:
                    residual(b - 1, 0, part)
                    statistics(b - 1, 0)
                maxima(b, 3, (b - 1, 0) if tail else None)
                if part != "last":
                    mask_low(b + 1)
                if tail:
                    residual(b - 1, 1, part)
                    times_gamma(b - 1, 0)
                if part != "last":
                    q_low(b + 1, 0, bank_of("Q0", part))
                if tail:
                    statistics(b - 1, 1)
                if part != "last":
                    pair_of_steps(b, part)

            pair_of_steps(-1, "lead")
            iteration(0, "first")
            with dve.Fori(1, B - 1) as b:
                iteration(b, "loop")
            iteration(B - 1, "last")
            b = B - 1
            reciprocals(b, (b - 1, 1), chunks=3)
            split_reciprocals(b, 0)
            residual(b - 1, 2, "last")
            residual(b - 1, 3, "last")
            normalise(b, 0, "last")
            normalise(b, 1, "last")
            end_low(b, 0)
            statistics(b - 1, 2)
            normalise(b, 2, "last", (b - 1, 2))
            statistics(b - 1, 3)
            reciprocals(b, (b - 1, 3), second=1)
            split_reciprocals(b, 1)
            times_gamma(b - 1, 1)
            normalise(b, 3, "last")
            times_gamma(b - 1, 2)
            end_low(b, 3)
            times_gamma(b - 1, 3)
            for t in range(NC):
                dve.wait_ge(last_out_done, t + 1)
                if t:
                    dve.wait_ge(stats_done, 4 * b + t)
                v.bn_stats(stats[:, t, :], ps_s[:, t, :]).then_inc(stats_done, 1)
                if t:
                    mean_of(t - 1)
                    times_gamma(b, t - 1, src=ps_s)
            dve.wait_ge(stats_done, 4 * b + 4)
            mean_of(3)
            times_gamma(b, 3, src=ps_s)
            for t in (2, 3):
                dve.wait_ge(scaled, 4 * b + t + 1)
                v.tensor_tensor(y[:, t, :], y[:, t, :], beta_sb[:], ALU.add).then_inc(end_y_ready, 1)

        @block.gpsimd
        def _(pool):
            gp = nc.gpsimd

            def k_blocks(b, c):
                kv = slice(KPC * c, KPC * (c + 1))
                head = const[:, C_HEAD:C_HEAD + GRP].rearrange("p (o g r) -> p o g r", o=1, r=1).broadcast_to([P, KPC, GRP, S])
                for part in range(2):
                    src = k_rep[:, b, part, kv, :] if isinstance(b, int) else \
                        k_rep[:, bass.ds(b, 1), part, kv, :].rearrange("p o h s -> p (o h) s")
                    last = gp.tensor_tensor(k_blk[:, part, kv, :, :],
                                            src.rearrange("p h (o s) -> p h o s", o=1).broadcast_to([P, KPC, GRP, S]),
                                            head, ALU.mult)
                last.then_inc(k_ready, 1)

            def v_blocks(b):
                src = v_rows[:, b, :] if isinstance(b, int) else v_rows[:, bass.ds(b, 1), :].rearrange("p o n -> p (o n)")
                half = const[:, C_HALF:C_HALF + 2].rearrange("p (o h r) -> p o h r", o=1, r=1).broadcast_to([P, KVH, 2, HD])
                gp.tensor_tensor(v_blk[:], src.rearrange("p (k o d) -> p k o d", k=KVH, o=1).broadcast_to([P, KVH, 2, HD]),
                                 half, ALU.mult).then_inc(v_ready, 1)

            def x_low(b, k):
                pool.wait_ge(x_hi_ready, 4 * b + k + 1)
                gp.tensor_tensor(x_lo[:, k, :], xt_raw[:, k, :], x_hi[:, k, :].bitcast(F32), ALU.subtract).then_inc(x_lo_ready, 1)

            def rsum_low(b):
                pool.wait_ge(rsum_hi_done, b + 1)
                gp.tensor_tensor(rsum_lo[:, 0, :], rsum[:, 0, :], rsum_hi[:, 0, :].bitcast(F32), ALU.subtract).then_inc(rsum_ready, 1)

            def o_low(bt, c):
                pool.wait_ge(o_hi_ready, 4 * bt + c + 1)
                gp.tensor_tensor(o_lo[:, c, :], o_sb[:, c, :], o_hi[:, c, :].bitcast(F32), ALU.subtract).then_inc(o_lo_ready, 1)

            def add_bo(bt, t, place=res_x):
                if place is res_x:
                    pool.wait_ge(res_in[t], 16 * (bt + 2))
                else:
                    pool.wait_ge(last_x_in[t], 16)
                gp.tensor_tensor(place[:, t, :], place[:, t, :], bo_sb[:], ALU.add).then_inc(res_ready, 1)

            def inv_std(bt, t):
                m = 4 * bt + t + 1
                pool.wait_ge(mean_done, m)
                gp.tensor_tensor(var_eps[:, t:t + 1], mean_var[:, t, 1:2], eps[:], ALU.add).then_inc(eps_done, 1)
                pool.wait_ge(eps_done, m)
                gp.tensor_tensor(rstd[:, t:t + 1], var_eps[:, t:t + 1], neg_half[:], ALU.pow).then_inc(rstd_done, 1)

            def add_beta(bt, t):
                pool.wait_ge(scaled, 4 * bt + t + 1)
                gp.tensor_tensor(y[:, t, :], y[:, t, :], beta_sb[:], ALU.add).then_inc(y_ready, 1)

            gp.memset(max_cols[:], 0.0).then_inc(zeroed, 1)
            gp.memset(oth_max[:], 0.0).then_inc(zeroed, 1)
            gp.memset(eps[:], EPS).then_inc(zeroed, 1)
            gp.memset(neg_half[:], -0.5).then_inc(zeroed, 1)
            for k in range(3):
                x_low(0, k)
            pool.wait_ge(const_in, 16)
            for c in range(NC):
                if c % 2 == 0:
                    pool.wait_ge(rep_copied_a, 1 + c // 2)
                    pool.wait_ge(rep_copied_d, 1 + c // 2)
                if c == 2:
                    pool.wait_ge(v_copied, 1)
                    v_blocks(0)
                k_blocks(0, c)
                if c == 0:
                    x_low(0, 3)
            pool.wait_ge(v_copied, 2)
            pool.wait_ge(zeroed, 4)
            pool.wait_ge(vec_in, 3 * 16)

            def blocks(b, c):
                pool.wait_ge(scores_done, 8 * b + 2 * c + 2)
                k_blocks(b + 1, c)

            def pair_of_steps(b, part):
                tail = part == "loop"
                blocks(b, 2)
                if tail:
                    inv_std(b - 1, 1)
                    add_beta(b - 1, 1)
                pool.wait_ge(pv_done, 4 * b + 4)
                v_blocks(b + 1)
                rsum_low(b)
                if tail:
                    inv_std(b - 1, 2)
                blocks(b, 3)
                o_low(b, 0)
                if tail:
                    inv_std(b - 1, 3)
                for c in range(1, NC):
                    o_low(b, c)
                if tail:
                    add_beta(b - 1, 2)
                    add_beta(b - 1, 3)

            def iteration(b, part):
                tail = part != "first"
                if tail:
                    add_bo(b - 1, 0)
                    add_bo(b - 1, 1)
                if part != "last":
                    blocks(b, 0)
                if part != "last":
                    for k in range(NC):
                        x_low(b + 1, k)
                    blocks(b, 1)
                if tail:
                    add_bo(b - 1, 2)
                    add_bo(b - 1, 3)
                    inv_std(b - 1, 0)
                if part == "last":
                    for t in range(NC):
                        add_bo(b, t, xt_raw)
                if tail:
                    add_beta(b - 1, 0)
                else:
                    for k in range(NC):
                        pool.wait_ge(wo_hi_ready, k + 1)
                        gp.tensor_tensor(wo_lo[:, k, :], res_x[:, k, :], wo_hi[:, k, :].bitcast(F32),
                                         ALU.subtract).then_inc(wo_lo_ready, 1)
                if part != "last":
                    pair_of_steps(b, part)

            iteration(0, "first")
            with pool.Fori(1, B - 1) as b:
                iteration(b, "loop")
            iteration(B - 1, "last")
            b = B - 1
            inv_std(b - 1, 1)
            o_low(b, 1)
            inv_std(b - 1, 2)
            o_low(b, 2)
            inv_std(b - 1, 3)
            for t in (1, 2, 3):
                add_beta(b - 1, t)
            inv_std(b, 0)
            inv_std(b, 1)
            add_beta(b, 0)
            inv_std(b, 2)
            add_beta(b, 1)
            inv_std(b, 3)


def constants():
    c = np.zeros((P, C_ALL), np.float32)
    r = np.arange(P)
    c[r, C_ID + r] = 1
    for j in range(PAIRS):
        for h in range(2):
            for part in range(3):
                c[64 * h + 3 * j + part, C_MAX + j * P + 64 * h:C_MAX + j * P + 64 * (h + 1)] = -1
    for part in range(2):
        for h in range(2):
            c[part * S + np.arange(S), C_MASK + h * S + np.arange(S)] = 1
    for chunk in range(NC):
        for pair in range(PAIRS):
            for h in range(2):
                row, col = BLK * pair + 2 * chunk + h, BLK * pair + HD * h
                c[row, C_SPREAD + chunk * P + col:C_SPREAD + chunk * P + col + HD] = 1
        for m in range(BLK):
            head = slice(S * (m % 2), S * (m % 2 + 1))
            if m % 8 // 2 == chunk:
                c[head, C_SUM + chunk * BLK + m] = 1
            if m % 8 // 2 >= NC - 2:
                c[head, C_SUM + NC * BLK + m] = 1
            c[head, C_SUM + (NC + 1) * BLK + m] = 1
    for g in range(GRP):
        c[:, C_HEAD + g] = (r % 64) // HD == g
    for h in range(2):
        c[:, C_HALF + h] = r // S == h
    return c


def kernel(x, ctx_2048, mask_Bx1xSxS2_ff0, L0_xattn_Wq, L0_xattn_bq, L0_xattn_Wk, L0_xattn_bk, L0_xattn_Wv,
           L0_xattn_bv, L0_xattn_Wo, L0_xattn_bo, L0_xattn_gamma, L0_xattn_beta):
    import concourse.bacc as bacc
    from concourse.bass_utils import run_bass_kernel_spmd

    x = np.asarray(x)
    arrays = {
        "x_t": x.transpose(0, 2, 1).reshape(B, NC, P, L),
        "x_n": x.reshape(B * L, D),
        "ctx_t": np.asarray(ctx_2048).reshape(B, S, NC, P).transpose(3, 2, 0, 1).reshape(P, NC, B * S),
        "mask_t": np.asarray(mask_Bx1xSxS2_ff0).reshape(B, L, S).transpose(0, 2, 1),
        "wq": np.asarray(L0_xattn_Wq),
        "bq": np.asarray(L0_xattn_bq).reshape(NC, P).T,
        "wk": np.asarray(L0_xattn_Wk),
        "bk": np.asarray(L0_xattn_bk).reshape(P, 1),
        "wv": np.asarray(L0_xattn_Wv),
        "bv": np.asarray(L0_xattn_bv),
        "wo": np.asarray(L0_xattn_Wo),
        "bo": np.asarray(L0_xattn_bo),
        "gamma": np.asarray(L0_xattn_gamma),
        "beta": np.asarray(L0_xattn_beta),
        "consts": constants(),
    }
    arrays = {name: np.ascontiguousarray(a) for name, a in arrays.items()}
    nc = bacc.Bacc("TRN2", target_bir_lowering=False, num_devices=1)
    args = {name: nc.dram_tensor(name, a.shape, mybir.dt.from_np(a.dtype), kind="ExternalInput").ap()
            for name, a in arrays.items()}
    out = nc.dram_tensor("out", (B * L, D), F32, kind="ExternalOutput").ap()
    cross_attention(nc, out=out, **args)
    result = run_bass_kernel_spmd(nc, [arrays], core_ids=[0])
    return result.results[0]["out"].reshape(B, L, D)
```

```python
from contextlib import ExitStack

import numpy as np

import concourse.bass as bass
from concourse import mybir

ALU = mybir.AluOpType
ACT = mybir.ActivationFunctionType
AX = mybir.AxisListType
F32 = mybir.dt.float32
F32R = mybir.dt.float32r
BF16 = mybir.dt.bfloat16

P = 128
B, L, S, D = 4, 512, 64, 512
NH, KVH = 32, 8
HD = D // NH
NC = D // P
HPC = NH // NC
KPC = KVH // NC
PAIRS = HPC // 2
GRP = NH // KVH
BLK = 32
NB = L // BLK
EPS = 1e-6
WARM_UP = 9
SCALE = 0.25

C_ID, C_HEAD = 0, P
C_HALF = C_HEAD + GRP
C_PART = C_HALF + 2
C_EARLY = C_PART + 1
C_MASK, C_SPREAD = C_EARLY, C_EARLY + P
C_MAX = C_SPREAD + NC * P
C_SUM = C_MAX + PAIRS * P
C_ALL = C_SUM + (NC + 2) * BLK

ITEMS = {
    "lead": ["Q0", "Q1", "Q2"],
    "first": ["Q3", "Q0", "Q1", "Q2", "R0", "R1", "R2"],
    "loop": ["P3", "Q3", "O0", "Q0", "Q1", "O1", "Q2", "O2", "O3", "R0", "R1", "R2"],
    "last": ["P3", "Q3", "O0", "O1", "O2", "R0", "R1", "O3", "R2", "R3"],
}
BEFORE = len(ITEMS["lead"]) + len(ITEMS["first"])
PER_LOOP = len(ITEMS["loop"])


def item(b, name, part):
    at = ITEMS[part].index(name)
    if part == "lead":
        return at
    if part == "first":
        return len(ITEMS["lead"]) + at
    return PER_LOOP * b - PER_LOOP + BEFORE + at


def bank_of(name, part):
    return item(1, name, part) % 2


def cross_attention(nc, x_t, x_n, ctx_t, mask_t, wq, bq, wk, bk, wv, bv, wo, bo, gamma, beta, consts, out):
    with ExitStack() as ctx:
        def sb(name, shape, dt=F32):
            return ctx.enter_context(nc.sbuf_tensor(name, shape, dt))

        def sem(name):
            return ctx.enter_context(nc.semaphore(name))

        const = sb("const", [P, C_ALL])
        const_r = sb("const_r", [P, C_MAX - C_EARLY], F32R)
        ctx_sb = sb("ctx_sb", [P, NC, B * S])
        wk_sb = sb("wk_sb", [P, NC, P])
        wv_sb = sb("wv_sb", [P, NC, P])
        bq_sb = sb("bq_sb", [P, NC])
        bk_sb = sb("bk_sb", [P, 1])
        bv_sb = sb("bv_sb", [P, P])
        bo_sb = sb("bo_sb", [P, D])
        gamma_sb = sb("gamma_sb", [P, D])
        beta_sb = sb("beta_sb", [P, D])
        wq_hi = sb("wq_hi", [P, NC, D], F32R)
        wq_lo = sb("wq_lo", [P, NC, D], F32R)
        wo_hi = sb("wo_hi", [P, NC, D], F32R)
        wo_lo = sb("wo_lo", [P, NC, D], F32R)
        xt_raw = sb("xt_raw", [P, NC, L])
        x_hi = sb("x_hi", [P, NC, L], F32R)
        x_lo = sb("x_lo", [P, NC, L], F32R)
        kt = sb("kt", [P, B * S])
        kt_hi = sb("kt_hi", [P, B * S], F32R)
        kt_lo = sb("kt_lo", [P, B * S], F32R)
        k_rep = sb("k_rep", [P, B, 2, KVH, S])
        k_blk = sb("k_blk", [P, 2, KVH, GRP, S], F32R)
        v_rows = sb("v_rows", [P, B, P])
        v_blk = sb("v_blk", [P, KVH, 2, HD])
        mask_raw = sb("mask_raw", [P, L])
        mask_rnd = sb("mask_rnd", [P, L], F32R)
        mask_parts = sb("mask_parts", [P, L], F32R)
        q_parts = sb("q_parts", [P, 2, 2, L], F32R)
        blk_max = sb("blk_max", [P, PAIRS, NB])
        oth_max = sb("oth_max", [P, PAIRS, NB])
        tok_max = sb("tok_max", [P, PAIRS, NB])
        max_rest = sb("max_rest", [P, PAIRS, NB])
        max_cols = sb("max_cols", [P, NB, BLK], BF16)
        max_rows = sb("max_rows", [P, L], BF16)
        neg_pick = sb("neg_pick", [P, PAIRS * P], BF16)
        probs = sb("probs", [P, 2, PAIRS, L])
        o_sb = sb("o_sb", [P, NC, L])
        rsum = sb("rsum", [P, 2, L])
        rsum_hi = sb("rsum_hi", [P, 2, L], F32R)
        rsum_parts = sb("rsum_parts", [P, 2, L], F32R)
        o_hi = sb("o_hi", [P, NC, L], F32R)
        o_lo = sb("o_lo", [P, NC, L], F32R)
        res_x = sb("res_x", [P, NC, D])
        y = sb("y", [P, NC, D])
        stats = sb("stats", [P, NC, 6])
        mean_var = sb("mean_var", [P, NC, 2])
        var_eps = sb("var_eps", [P, NC])
        rstd = sb("rstd", [P, NC])
        mean_rstd = sb("mean_rstd", [P, NC])
        neg_shift = sb("neg_shift", [P, NC])
        eps = sb("eps", [P, 2])
        neg_half = sb("neg_half", [P, 2])
        neg_one = sb("neg_one", [P, 2])

        ps_s = ctx.enter_context(nc.psum_tensor("ps_s", [P, PAIRS, L], F32))
        ps_o = ctx.enter_context(nc.psum_tensor("ps_o", [P, L], F32))
        ps_z = ctx.enter_context(nc.psum_tensor("ps_z", [P, L], F32))
        ps_w = ctx.enter_context(nc.psum_tensor("ps_w", [P, 2, L], F32))

        k_in = sem("k_in")
        early_in = sem("early_in")
        const_in = sem("const_in")
        bk_in = sem("bk_in")
        bq_in = sem("bq_in")
        v_in = sem("v_in")
        vec_in = sem("vec_in")
        y_dma = [sem(f"y_dma{t}") for t in range(NC)]
        res_in = [sem(f"res_in{t}") for t in range(NC)]
        last_x_in = [sem(f"last_x_in{t}") for t in range(NC)]
        x_in = [sem(f"x_in{k}") for k in range(NC)]
        mask_in = sem("mask_in")
        zeroed = sem("zeroed")
        pick_ready = sem("pick_ready")
        const_rounded = sem("const_rounded")
        neg_pick_ready = sem("neg_pick_ready")
        kt_done = sem("kt_done")
        kt_added = sem("kt_added")
        kt_split = sem("kt_split")
        rep_done = sem("rep_done")
        rep_copied_a = sem("rep_copied_a")
        rep_copied_d = sem("rep_copied_d")
        v_done = sem("v_done")
        v_copied = sem("v_copied")
        wq_hi_ready = sem("wq_hi_ready")
        wq_lo_ready = sem("wq_lo_ready")
        wo_hi_ready = sem("wo_hi_ready")
        wo_lo_ready = sem("wo_lo_ready")
        x_hi_ready = sem("x_hi_ready")
        x_lo_ready = sem("x_lo_ready")
        k_ready = sem("k_ready")
        v_ready = sem("v_ready")
        mask_rounded = sem("mask_rounded")
        mask_ready = sem("mask_ready")
        scores_done = sem("scores_done")
        max_done = sem("max_done")
        oth_copied = sem("oth_copied")
        max_top_done = sem("max_top_done")
        max_mid_done = sem("max_mid_done")
        max_low_done = sem("max_low_done")
        max_ready = sem("max_ready")
        shifted = sem("shifted")
        exp_done = sem("exp_done")
        pv_done = sem("pv_done")
        o_copied = sem("o_copied")
        z_read = sem("z_read")
        rsum_hi_done = sem("rsum_hi_done")
        rsum_ready = sem("rsum_ready")
        item_done = sem("item_done")
        placed = sem("placed")
        last_out_done = sem("last_out_done")
        q_read = sem("q_read")
        q_hi_done = sem("q_hi_done")
        norm_done = sem("norm_done")
        o_hi_ready = sem("o_hi_ready")
        o_lo_ready = sem("o_lo_ready")
        o_lo3_ready = sem("o_lo3_ready")
        res_ready = sem("res_ready")
        resid_done = sem("resid_done")
        stats_done = sem("stats_done")
        mean_done = sem("mean_done")
        gamma_done = sem("gamma_done")
        product_done = sem("product_done")
        shift_done = sem("shift_done")
        gamma_mul = sem("gamma_mul")
        eps_done = sem("eps_done")
        rstd_done = sem("rstd_done")
        scaled = sem("scaled")
        y_ready = sem("y_ready")
        end_gamma = sem("end_gamma")
        end_y_ready = sem("end_y_ready")

        pick = o_hi[:, 0:KVH * P // L, :].rearrange("p c n -> p (c n)")

        block = ctx.enter_context(nc.Block())

        def last_store(engine, bt, t, place):
            engine.dma_start(out[(bt * NC + t) * P:(bt * NC + t + 1) * P, :], place[:, t, :]).then_inc(y_dma[t], 16)

        def row(a):
            return a.rearrange("(o n) -> o n", o=1)

        @block.sync
        def _(sp):
            sp.dma_start(ctx_sb[:], ctx_t).then_inc(k_in, 16)
            sp.dma_start(const[:, 0:C_EARLY], consts[:, 0:C_EARLY]).then_inc(early_in, 16)
            sp.dma_start(bk_sb[:], bk).then_inc(bk_in, 16)
            for k in range(NC):
                sp.dma_start(xt_raw[:, k, :], x_t[0, k]).then_inc(x_in[k], 16)
            sp.dma_start(bq_sb[:], bq).then_inc(bq_in, 16)
            for h in range(2):
                sp.dma_start(mask_raw[h * S:(h + 1) * S, :], mask_t[0]).then_inc(mask_in, 16)
            sp.dma_start(const[:, C_EARLY:C_ALL], consts[:, C_EARLY:C_ALL]).then_inc(const_in, 16)
            sp.dma_start(wv_sb[:], wv.rearrange("(k p) n -> p k n", p=P)).then_inc(v_in, 16)
            sp.dma_start(bv_sb[:], row(bv).broadcast_to([P, P])).then_inc(v_in, 16)
            sp.dma_start(bo_sb[:], row(bo).broadcast_to([P, D])).then_inc(vec_in, 16)
            sp.dma_start(gamma_sb[:], row(gamma).broadcast_to([P, D])).then_inc(vec_in, 16)
            sp.dma_start(beta_sb[:], row(beta).broadcast_to([P, D])).then_inc(vec_in, 16)
            for t in range(NC):
                sp.dma_start(res_x[:, t, :], wo[t * P:(t + 1) * P, :]).then_inc(res_in[t], 16)

            def store(bt, t):
                sp.wait_ge(y_ready, 4 * bt + t + 1)
                sp.dma_start(out[bass.ds((bt * NC + t) * P, P), :], y[:, t, :]).then_inc(y_dma[t], 16)

            def load_next(b):
                sp.wait_ge(x_lo_ready, 4 * b + 4)
                for k in range(NC):
                    sp.dma_start(xt_raw[:, k, :], x_t[b + 1, k] if isinstance(b, int) else
                                 x_t[bass.ds(b + 1, 1), k].rearrange("o p n -> (o p) n")).then_inc(x_in[k], 16)
                sp.wait_ge(mask_ready, b + 1)
                for h in range(2):
                    sp.dma_start(mask_raw[h * S:(h + 1) * S, :], mask_t[b + 1] if isinstance(b, int) else
                                 mask_t[bass.ds(b + 1, 1)].rearrange("o p n -> (o p) n")).then_inc(mask_in, 16)

            def tails(b):
                for t in range(NC):
                    sp.wait_ge(resid_done, 4 * b - 4 + t + 1)
                    sp.dma_start(res_x[:, t, :], x_n[bass.ds((b * NC + t) * P, P), :]).then_inc(res_in[t], 16)
                    store(b - 1, t)

            load_next(0)
            load_next(1)
            for t in range(NC):
                sp.wait_ge(wo_lo_ready, t + 1)
                sp.dma_start(res_x[:, t, :], x_n[t * P:(t + 1) * P, :]).then_inc(res_in[t], 16)
            with sp.Fori(1, B - 2) as b:
                load_next(b + 1)
                tails(b)
            sp.wait_ge(x_lo_ready, 4 * B)
            for t in range(NC):
                sp.dma_start(xt_raw[:, t, :], x_n[((B - 1) * NC + t) * P:((B - 1) * NC + t + 1) * P, :]).then_inc(last_x_in[t], 16)
            tails(B - 2)

            for t in range(NC):
                if t < 3:
                    store(B - 2, t)
                else:
                    sp.wait_ge(end_y_ready, 1)
                    last_store(sp, B - 2, t, y)
            for t in range(1, NC):
                sp.wait_ge(end_y_ready, 1 + t)
                last_store(sp, B - 1, t, res_x)
            for t in range(NC):
                sp.wait_ge(y_dma[t], 16 * (B + 1))

        @block.tensor
        def _(pe):
            mm = nc.tensor.matmul

            def q_item(b, c, bank, free=None, halfway=None):
                dst = ps_w[:, bank, :]
                if free:
                    pe.wait_ge(*free)
                for k in range(NC):
                    if halfway and k == 2:
                        halfway()
                    if c == 0:
                        if isinstance(b, int) and b == 0:
                            pe.wait_ge(wq_lo_ready, k + 1)
                        pe.wait_ge(x_lo_ready, 4 * b + k + 1)
                    wh = wq_hi[:, k, c * P:(c + 1) * P]
                    wl = wq_lo[:, k, c * P:(c + 1) * P]
                    mm(dst, wh, x_hi[:, k, :], start=k == 0, stop=False)
                    mm(dst, wh, x_lo[:, k, :], start=False, stop=False)
                    last = mm(dst, wl, x_hi[:, k, :], start=False, stop=k == NC - 1)
                last.then_inc(item_done, 1)

            def spread_item(bt, c, bank, free=None, second=0):
                pe.wait_ge(rsum_ready, bt + 1 + second)
                if free:
                    pe.wait_ge(*free)
                sel = const_r[:, C_SPREAD - C_EARLY + c * P:C_SPREAD - C_EARLY + (c + 1) * P]
                mm(ps_w[:, bank, :], sel, rsum_parts[:, second, :], start=True, stop=True).then_inc(item_done, 1)

            def out_products(dst, c, t, first=True, hi=o_hi, lo=o_lo):
                oh = hi[:, c, t * P:(t + 1) * P]
                ol = lo[:, c, t * P:(t + 1) * P]
                mm(dst, oh, wo_hi[:, c, :], start=first and c == 0, stop=False, skip_group_check=True)
                mm(dst, oh, wo_lo[:, c, :], start=False, stop=False, skip_group_check=True)
                return mm(dst, ol, wo_hi[:, c, :], start=False, stop=c == NC - 1, skip_group_check=True)

            def out_item(bt, t, bank, free=None):
                if free:
                    pe.wait_ge(*free)
                pe.wait_ge(o_lo_ready, 3 * bt + 3)
                pe.wait_ge(o_lo3_ready, bt + 1)
                for c in range(NC):
                    last = out_products(ps_w[:, bank, :], c, t)
                last.then_inc(item_done, 1)

            def scores(b, c):
                i = 4 * b + c
                pe.wait_ge(q_read, i + 1)
                pe.wait_ge(k_ready, i + 1)
                if c == 0:
                    pe.wait_ge(mask_ready, b + 1)
                for j in range(PAIRS):
                    if j % 2 == 0 and not (isinstance(i, int) and i == 0):
                        pe.wait_ge(exp_done, 2 * i - 1 + j // 2)
                    kv, g = KPC * c + j // 2, 2 * (j % 2)
                    q = q_parts[:, c % 2, j // 2, :]
                    mm(ps_s[:, j, :], k_blk[:, 0, kv, g:g + 2, :], q, start=True, stop=False, skip_group_check=True)
                    mm(ps_s[:, j, :], k_blk[:, 1, kv, g:g + 2, :], q, start=False, stop=False, skip_group_check=True)
                    last = mm(ps_s[:, j, :], const_r[:, C_MASK - C_EARLY:C_MASK - C_EARLY + P], mask_parts[:],
                              start=False, stop=True, skip_group_check=True)
                    if j % 2 == 1:
                        last.then_inc(scores_done, 1)

            def shift(b, c):
                if isinstance(b, int) and b == 0 and c == 0:
                    pe.wait_ge(neg_pick_ready, 1)
                pe.wait_ge(max_ready, 4 * b + c + 1)
                for j in range(PAIRS):
                    last = mm(ps_s[:, j, :], neg_pick[:, j * P:(j + 1) * P], max_rows[:],
                              start=False, stop=True, skip_group_check=True)
                    if j % 2 == 1:
                        last.then_inc(shifted, 1)

            def outputs(b, c):
                i = 4 * b + c
                pe.wait_ge(exp_done, 2 * i + 2)
                if not (isinstance(i, int) and i == 0):
                    pe.wait_ge(o_copied, i)
                if c == 0:
                    pe.wait_ge(v_ready, b + 1)
                for j in range(PAIRS):
                    mm(ps_o[BLK * j:BLK * (j + 1), :], v_blk[:, KPC * c + j // 2, :, :], probs[:, c % 2, j, :],
                       start=True, stop=True)

            def sums(b, c, split=False):
                if c == 0 and isinstance(b, int) and b == 0:
                    pe.wait_ge(v_copied, 2)
                elif c == 0:
                    pe.wait_ge(z_read, b)
                if split and c == 3:
                    pe.wait_ge(z_read, b + 1)
                rows = c + 2 if split and c >= 2 else c
                for j in range(PAIRS):
                    last = mm(ps_z[BLK * j:BLK * (j + 1), :], const[:, C_SUM + rows * BLK:C_SUM + (rows + 1) * BLK],
                              probs[:, c % 2, j, :], start=c == 0 or split and c == 3,
                              stop=c == NC - 1 or split and c == 2, skip_group_check=True)
                last.then_inc(pv_done, 1)

            pe.wait_ge(zeroed, 1)
            zeros = max_cols[:].rearrange("p n e -> p (n e)")
            for _ in range(WARM_UP):
                mm(ps_w[:, 0, :], zeros[:, 0:P], zeros, start=True, stop=True)

            pe.wait_ge(k_in, 2 * 16)
            for k in range(NC):
                last = mm(ps_o[:, 0:B * S], wk_sb[:, k, :], ctx_sb[:, k, :], start=k == 0, stop=k == NC - 1)
            last.then_inc(kt_done, 1)

            def v_item(b):
                if b == 0:
                    pe.wait_ge(v_in, 2 * 16)
                if b == 2:
                    pe.wait_ge(v_copied, 1)
                for k in range(NC):
                    for h in range(2):
                        last = mm(ps_z[h * S:(h + 1) * S, b * P:(b + 1) * P], ctx_sb[:, k, b * S:(b + 1) * S],
                                  wv_sb[:, k, :], start=k == 0, stop=k == NC - 1)
                last.then_inc(v_done, 1)

            def replicate(half):
                for part, parts in enumerate((kt_hi, kt_lo)):
                    if half == 0:
                        pe.wait_ge(kt_split, part + 1)
                    elif part:
                        pe.wait_ge(rep_copied_d, 1)
                    else:
                        pe.wait_ge(rep_copied_a, 1)
                    for i in range(KVH // 2):
                        kv = half * KVH // 2 + i
                        last = mm(ps_s[:, 2 * part + i // 2, (i % 2) * B * S:(i % 2 + 1) * B * S],
                                  pick[:, kv * P:(kv + 1) * P], parts[:], start=True, stop=True)
                last.then_inc(rep_done, 1)

            pe.wait_ge(pick_ready, 1)
            replicate(0)
            q_item(0, 0, bank_of("Q0", "lead"), halfway=lambda: replicate(1))
            pe.wait_ge(const_rounded, 1)
            pe.wait_ge(rep_copied_a, 2)
            pe.wait_ge(rep_copied_d, 2)

            def pair_of_steps(b, part):
                tail = part == "loop"
                if part == "lead":
                    v_item(0)
                    v_item(1)
                scores(b + 1, 0)
                q_item(b + 1, 1, bank_of("Q1", part), (resid_done, 4 * b - 3) if tail else None)
                if tail:
                    out_item(b - 1, 1, bank_of("O1", part))
                elif part == "lead":
                    v_item(2)
                else:
                    outputs(b, 3)
                    sums(b, 3)
                shift(b + 1, 0)
                if tail:
                    outputs(b, 3)
                    sums(b, 3)
                if part == "lead":
                    v_item(3)
                scores(b + 1, 1)
                q_item(b + 1, 2, bank_of("Q2", part))
                if tail:
                    out_item(b - 1, 2, bank_of("O2", part), (resid_done, 4 * b - 2))
                else:
                    outputs(b + 1, 0)
                shift(b + 1, 1)
                if tail:
                    outputs(b + 1, 0)
                    out_item(b - 1, 3, bank_of("O3", part), (q_read, 4 * b + 7))
                if part != "lead":
                    spread_item(b, 0, bank_of("R0", part), (resid_done, 4 * b - 1) if tail else None)
                sums(b + 1, 0)
                if part != "lead":
                    spread_item(b, 1, bank_of("R1", part), (resid_done, 4 * b) if tail else (q_read, 4 * b + 7))
                    spread_item(b, 2, bank_of("R2", part), (norm_done, 4 * b + 1))

            def iteration(b, part):
                tail = part != "first"
                scores(b, 2)
                if tail:
                    spread_item(b - 1, 3, bank_of("P3", part), (norm_done, 4 * b - 2))
                q_item(b, 3, bank_of("Q3", part), (norm_done, 4 * b - 1) if tail else None)
                outputs(b, 1)
                shift(b, 2)
                sums(b, 1)
                scores(b, 3)
                if tail:
                    out_item(b - 1, 0, bank_of("O0", part))
                if part == "last":
                    out_item(b - 1, 1, bank_of("O1", part))
                else:
                    q_item(b + 1, 0, bank_of("Q0", part))
                if not tail:
                    outputs(b, 2)
                shift(b, 3)
                if tail:
                    outputs(b, 2)
                sums(b, 2, split=part == "last")
                if part != "last":
                    pair_of_steps(b, part)

            pair_of_steps(-1, "lead")
            iteration(0, "first")
            pe.wait_ge(wo_lo_ready, NC)
            with pe.Fori(1, B - 1) as b:
                iteration(b, "loop")
            iteration(B - 1, "last")
            b = B - 1
            out_item(b - 1, 2, bank_of("O2", "last"), (resid_done, 4 * b - 3))
            outputs(b, 3)
            sums(b, 3, split=True)
            spread_item(b, 0, bank_of("R0", "last"), (resid_done, 4 * b - 2))
            spread_item(b, 1, bank_of("R1", "last"), (resid_done, 4 * b - 1))
            out_item(b - 1, 3, bank_of("O3", "last"), (norm_done, 4 * b + 1))
            spread_item(b, 2, bank_of("R2", "last"), (norm_done, 4 * b + 2))
            for c, tiles in [(0, range(NC)), (1, range(NC))] + [(c, (t,)) for t in range(NC) for c in (2, 3)]:
                if tiles[0] == 0:
                    if c < 3:
                        pe.wait_ge(o_lo_ready, 3 * b + c + 1)
                    else:
                        pe.wait_ge(o_lo3_ready, b + 1)
                for t in tiles:
                    if c == 0:
                        pe.wait_ge(placed, t + 1)
                    last = out_products(ps_s[:, t, :], c, t, first=False, hi=x_hi, lo=x_lo)
                    if c == 3:
                        last.then_inc(last_out_done, 1)
                    if c == 1 and t == 0:
                        spread_item(b, 3, bank_of("R3", "last"), (resid_done, 4 * b), second=1)

        @block.scalar
        def _(act):
            act.dma_start(wk_sb[:], wk.rearrange("(k p) n -> p k n", p=P)).then_inc(k_in, 16)
            for k in range(NC):
                act.dma_start(y[:, k, :], wq[k * P:(k + 1) * P, :]).then_inc(y_dma[k], 16)
            go = nc.scalar.activation

            def x_high(b, k):
                act.wait_ge(x_in[k], 16 * (b + 1))
                go(x_hi[:, k, :], xt_raw[:, k, :], ACT.Copy).then_inc(x_hi_ready, 1)

            def mask_round(b):
                act.wait_ge(mask_in, 32 * (b + 1))
                go(mask_parts[0:S, :], mask_raw[0:S, :], ACT.Copy)
                go(mask_rnd[S:P, :], mask_raw[S:P, :], ACT.Copy).then_inc(mask_rounded, 1)

            def q_high(b, c, n, bank):
                act.wait_ge(item_done, n + 1)
                for h in range(2):
                    r = slice(h * 64, h * 64 + 64)
                    go(q_parts[r, c % 2, h, :], ps_w[r, bank, :], ACT.Identity,
                       bias=bq_sb[r, c:c + 1]).then_inc(q_hi_done, 1)

            def exps(b, c):
                for g in range(2):
                    act.wait_ge(shifted, 2 * (4 * b + c) + g + 1)
                    go(probs[:, c % 2, 2 * g:2 * g + 2, :], ps_s[:, 2 * g:2 * g + 2, :], ACT.Exp).then_inc(exp_done, 1)

            def copy_out(b, c, again):
                act.wait_ge(pv_done, 4 * b + c + 1)
                if again and c < 3:
                    act.wait_ge(o_lo_ready, 3 * b - 3 + c + 1)
                elif again:
                    act.wait_ge(o_lo3_ready, b)
                go(o_sb[:, c, :], ps_o[:], ACT.Copy).then_inc(o_copied, 1)

            def rsum_high(b):
                act.wait_ge(z_read, b + 1)
                go(rsum_hi[:, 0, :], rsum[:, 0, :], ACT.Copy).then_inc(rsum_hi_done, 1)

            def o_high(bt, c, place=o_hi):
                act.wait_ge(norm_done, 4 * bt + c + 1)
                go(place[:, c, :], o_sb[:, c, :], ACT.Copy).then_inc(o_hi_ready, 1)

            def standardise(bt, t):
                act.wait_ge(shift_done, 4 * bt + t + 1)
                go(y[:, t, :], y[:, t, :], ACT.Identity, scale=rstd[:, t:t + 1],
                   bias=neg_shift[:, t:t + 1]).then_inc(scaled, 1)

            def scale(bt, t):
                act.wait_ge(gamma_done, t + 1)
                act.wait_ge(rstd_done, 4 * bt + t + 1)
                go(res_x[:, t, :], res_x[:, t, :], ACT.Copy, scale=rstd[:, t:t + 1]).then_inc(scaled, 1)

            act.wait_ge(zeroed, 4)
            go(var_eps[:, 0:1], eps[:, 0:1], ACT.Exp)
            act.wait_ge(early_in, 16)
            go(pick.rearrange("p (h o d) -> p h o d", h=KVH, d=HD),
               const[:, C_ID:C_ID + P].rearrange("p (h o d) -> p h o d", h=KVH, o=1).broadcast_to([P, KVH, P // HD, HD]),
               ACT.Copy).then_inc(pick_ready, 1)
            for k in range(NC):
                x_high(0, k)

            def copy_hi(half):
                act.wait_ge(rep_done, half + 1)
                kv = slice(half * KVH // 2, (half + 1) * KVH // 2)
                go(k_rep[:, :, 0, kv, :].rearrange("p b h s -> p h b s"),
                   ps_s[:, 0:2, :].rearrange("p k (e b s) -> p (k e) b s", e=2, b=B), ACT.Copy).then_inc(rep_copied_a, 1)

            copy_hi(0)
            mask_round(0)
            copy_hi(1)
            act.wait_ge(const_in, 16)
            go(const_r[:], const[:, C_EARLY:C_MAX], ACT.Copy).then_inc(const_rounded, 1)
            act.wait_ge(bq_in, 16)
            q_high(0, 0, item(0, "Q0", "lead"), bank_of("Q0", "lead"))
            go(neg_pick[:], const[:, C_MAX:C_MAX + PAIRS * P], ACT.Copy).then_inc(neg_pick_ready, 1)

            def pair_of_steps(b, part):
                tail = part == "loop"
                q_high(b + 1, 1, item(b, "Q1", part), bank_of("Q1", part))
                exps(b + 1, 0)
                if part != "lead":
                    copy_out(b, 3, again=tail)
                if tail:
                    standardise(b - 1, 0)
                if part != "lead":
                    rsum_high(b)
                q_high(b + 1, 2, item(b, "Q2", part), bank_of("Q2", part))
                exps(b + 1, 1)
                if tail:
                    standardise(b - 1, 1)
                if part != "lead":
                    o_high(b, 0)
                    o_high(b, 1)
                copy_out(b + 1, 0, again=part != "lead")
                if part != "lead":
                    o_high(b, 2)
                if tail:
                    standardise(b - 1, 2)
                    standardise(b - 1, 3)

            def iteration(b, part):
                tail = part != "first"
                q_high(b, 3, item(b, "Q3", part), bank_of("Q3", part))
                if tail:
                    o_high(b - 1, 3)
                exps(b, 2)
                copy_out(b, 1, again=tail)
                if part == "loop":
                    for k in range(NC):
                        x_high(b + 1, k)
                if part != "last":
                    act.wait_ge(scores_done, 8 * b + 8)
                    mask_round(b + 1)
                    q_high(b + 1, 0, item(b, "Q0", part), bank_of("Q0", part))
                exps(b, 3)
                copy_out(b, 2, again=tail)
                if part == "first":
                    for k in range(NC):
                        act.wait_ge(res_in[k], 16)
                        go(wo_hi[:, k, :], res_x[:, k, :], ACT.Copy).then_inc(wo_hi_ready, 1)
                if part != "last":
                    pair_of_steps(b, part)

            pair_of_steps(-1, "lead")
            iteration(0, "first")
            with act.Fori(1, B - 1) as b:
                iteration(b, "loop")
            iteration(B - 1, "last")
            for t in range(NC):
                act.wait_ge(res_ready, 4 * (B - 1) + t + 1)
                if t == 0:
                    act.wait_ge(exp_done, 8 * B)
                go(ps_s[:, t, :], xt_raw[:, t, :], ACT.Copy).then_inc(placed, 1)
            standardise(B - 2, 0)
            copy_out(B - 1, 3, again=True)
            for c in range(NC):
                o_high(B - 1, c, x_hi)
                if c == 1:
                    standardise(B - 2, 1)
            standardise(B - 2, 3)
            standardise(B - 2, 2)
            for t in range(NC):
                scale(B - 1, t)
            act.wait_ge(y_ready, 4 * (B - 1))
            last_store(act, B - 1, 0, res_x)

        @block.vector
        def _(dve):
            v = nc.vector

            def q_low(b, c, bank):
                for h in range(2):
                    r, o = slice(h * 64, h * 64 + 64), slice(64 - h * 64, 128 - h * 64)
                    dve.wait_ge(q_hi_done, 2 * (4 * b + c) + h + 1)
                    last = v.scalar_tensor_tensor(q_parts[o, c % 2, h, :], ps_w[r, bank, :], bq_sb[r, c:c + 1],
                                                  q_parts[r, c % 2, h, :].bitcast(F32), ALU.add, ALU.subtract)
                last.then_inc(q_read, 1)

            def maxima(b, c, tile=None):
                i = 4 * b + c
                cols = max_cols[:, :, 0:3 * PAIRS].rearrange("p n (j e) -> p j n e", e=3)
                for g in range(2):
                    dve.wait_ge(scores_done, 2 * i + g + 1)
                    if tile and g == 0:
                        dve.wait_ge(stats_done, 4 * tile[0] + tile[1] + 1)
                    v.tensor_reduce(blk_max[:, 2 * g:2 * g + 2, :], ps_s[:, 2 * g:2 * g + 2, :].rearrange(
                        "p j (n r) -> p j n r", r=BLK), AX.X, ALU.max, apply_transpose=True).then_inc(max_done, 1)
                    if tile and g == 0:
                        mean_of(tile[1])
                dve.wait_ge(max_done, 2 * i + 2)
                for h in range(2):
                    last = v.tensor_copy(oth_max[64 * h:64 * h + 32, :, :], blk_max[64 * h + 32:64 * h + 64, :, :])
                last.then_inc(oth_copied, 1)
                dve.wait_ge(oth_copied, i + 1)
                v.tensor_tensor(tok_max[:], blk_max[:], oth_max[:], ALU.max)
                v.tensor_tensor(cols[:, :, :, 0], blk_max[:], oth_max[:], ALU.max).then_inc(max_top_done, 1)
                dve.wait_ge(max_top_done, i + 1)
                v.tensor_tensor(max_rest[:], tok_max[:], cols[:, :, :, 0], ALU.subtract)
                v.tensor_tensor(cols[:, :, :, 1], tok_max[:], cols[:, :, :, 0], ALU.subtract).then_inc(max_mid_done, 1)
                dve.wait_ge(max_mid_done, i + 1)
                v.tensor_tensor(cols[:, :, :, 2], max_rest[:], cols[:, :, :, 1], ALU.subtract).then_inc(max_low_done, 1)
                dve.wait_ge(max_low_done, i + 1)
                v.transpose(max_rows[:], max_cols[:].rearrange("p n e -> p (n e)")).then_inc(max_ready, 1)

            def mask_low(b):
                dve.wait_ge(mask_rounded, b + 1)
                v.tensor_tensor(mask_parts[S:P, :], mask_raw[S:P, :], mask_rnd[S:P, :].bitcast(F32),
                                ALU.subtract).then_inc(mask_ready, 1)

            def reciprocals(b, tile=None, chunks=NC, second=0):
                dve.wait_ge(pv_done, 4 * b + chunks)
                if tile:
                    dve.wait_ge(stats_done, 4 * tile[0] + tile[1] + 1)
                v.reciprocal(rsum[:, second, :], ps_z[:]).then_inc(z_read, 1)
                if tile:
                    mean_of(tile[1])

            def round_reciprocals(b, second):
                dve.wait_ge(z_read, b + 1 + second)
                v.tensor_copy(rsum_hi[:, second, :], rsum[:, second, :]).then_inc(rsum_hi_done, 1)

            def split_reciprocals(b, second=0):
                dve.wait_ge(rsum_hi_done, b + 1 + second)
                v.scalar_tensor_tensor(rsum_parts[:, second, :], rsum_hi[:, second, :].bitcast(F32),
                                       const[:, C_PART:C_PART + 1], rsum[:, second, :],
                                       ALU.mult, ALU.add).then_inc(rsum_ready, 1)

            def o_low3(b, hi=o_hi, lo=o_lo):
                dve.wait_ge(o_hi_ready, 4 * b + 4)
                v.tensor_tensor(lo[:, 3, :], o_sb[:, 3, :], hi[:, 3, :].bitcast(F32), ALU.subtract).then_inc(o_lo3_ready, 1)

            def normalise(b, c, part, tile=None, own=False):
                n, bank = (item(b + 1, "P3", part), bank_of("P3", part)) if c == 3 and not own else \
                    (item(b, f"R{c}", part), bank_of(f"R{c}", part))
                dve.wait_ge(item_done, n + 1)
                dve.wait_ge(o_copied, 4 * b + c + 1)
                if tile:
                    dve.wait_ge(stats_done, 4 * tile[0] + tile[1] + 1)
                v.tensor_tensor(o_sb[:, c, :], ps_w[:, bank, :], o_sb[:, c, :],
                                ALU.mult).then_inc(norm_done, 1)
                if tile:
                    mean_of(tile[1])

            def residual(bt, t, part, tile=None):
                dve.wait_ge(item_done, item(bt + 1, f"O{t}", part) + 1)
                dve.wait_ge(res_ready, 4 * bt + t + 1)
                dve.wait_ge(y_dma[t], 16 * (bt + 1))
                if tile:
                    dve.wait_ge(stats_done, 4 * tile[0] + tile[1] + 1)
                v.tensor_tensor(y[:, t, :], ps_w[:, bank_of(f"O{t}", part), :], res_x[:, t, :], ALU.add).then_inc(resid_done, 1)
                if tile:
                    mean_of(tile[1])

            def statistics(bt, t):
                dve.wait_ge(resid_done, 4 * bt + t + 1)
                v.bn_stats(stats[:, t, :], y[:, t, :]).then_inc(stats_done, 1)

            def mean_of(t):
                v.bn_aggr(mean_var[:, t, :], stats[:, t, :]).then_inc(mean_done, 1)

            def times_gamma(bt, t):
                dve.wait_ge(mean_done, 4 * bt + t + 1)
                v.scalar_tensor_tensor(res_x[:, t, :], ps_s[:, t, :], mean_var[:, t, 0:1], gamma_sb[:],
                                       ALU.subtract, ALU.mult).then_inc(gamma_done, 1)

            def wq_split(k):
                dve.wait_ge(y_dma[k], 16)
                v.tensor_copy(wq_hi[:, k, :], y[:, k, :]).then_inc(wq_hi_ready, 1)
                dve.wait_ge(wq_hi_ready, k + 1)
                v.tensor_tensor(wq_lo[:, k, :], y[:, k, :], wq_hi[:, k, :].bitcast(F32), ALU.subtract).then_inc(wq_lo_ready, 1)

            def copy_lo(half):
                dve.wait_ge(rep_done, half + 1)
                kv = slice(half * KVH // 2, (half + 1) * KVH // 2)
                v.tensor_copy(k_rep[:, :, 1, kv, :].rearrange("p b h s -> p h b s"),
                              ps_s[:, 2:4, :].rearrange("p k (e b s) -> p (k e) b s", e=2, b=B)).then_inc(rep_copied_d, 1)

            def v_copy(half):
                dve.wait_ge(v_done, 2 * half + 2)
                b = slice(2 * half, 2 * half + 2)
                v.tensor_tensor(v_rows[:, b, :], ps_z[:].rearrange("p (b n) -> p b n", b=B)[:, b, :],
                                bv_sb[:].rearrange("p (o n) -> p o n", o=1).broadcast_to([P, 2, P]), ALU.add).then_inc(v_copied, 1)

            wq_split(0)
            dve.wait_ge(bk_in, 16)
            dve.wait_ge(kt_done, 1)
            v.tensor_scalar(kt[:], ps_o[:, 0:B * S], bk_sb[:], SCALE, ALU.add, ALU.mult).then_inc(kt_added, 1)
            dve.wait_ge(kt_added, 1)
            v.tensor_copy(kt_hi[:], kt[:]).then_inc(kt_split, 1)
            dve.wait_ge(kt_split, 1)
            v.tensor_tensor(kt_lo[:], kt[:], kt_hi[:].bitcast(F32), ALU.subtract).then_inc(kt_split, 1)
            wq_split(1)
            copy_lo(0)
            wq_split(2)
            wq_split(3)
            copy_lo(1)
            mask_low(0)
            dve.wait_ge(zeroed, 2)
            q_low(0, 0, bank_of("Q0", "lead"))

            def pair_of_steps(b, part):
                tail = part == "loop"
                if part == "lead":
                    dve.wait_ge(v_in, 2 * 16)
                    v_copy(0)
                maxima(b + 1, 0, (b - 1, 0) if tail else None)
                q_low(b + 1, 1, bank_of("Q1", part))
                if part == "lead":
                    v_copy(1)
                if tail:
                    residual(b - 1, 1, part)
                    statistics(b - 1, 1)
                if part != "lead":
                    reciprocals(b, (b - 1, 1) if tail else None)
                maxima(b + 1, 1)
                q_low(b + 1, 2, bank_of("Q2", part))
                if part != "lead":
                    split_reciprocals(b)
                if tail:
                    residual(b - 1, 2, part)
                    statistics(b - 1, 2)
                    residual(b - 1, 3, part, (b - 1, 2))
                if part != "lead":
                    normalise(b, 0, part)
                if tail:
                    statistics(b - 1, 3)
                if part != "lead":
                    normalise(b, 1, part)
                    normalise(b, 2, part, (b - 1, 3) if tail else None)

            def iteration(b, part):
                tail = part != "first"
                maxima(b, 2)
                if tail:
                    normalise(b - 1, 3, part)
                q_low(b, 3, bank_of("Q3", part))
                if tail:
                    o_low3(b - 1)
                else:
                    for k in range(NC):
                        dve.wait_ge(x_in[k], 16 * (b + 2))
                        v.tensor_copy(x_hi[:, k, :], xt_raw[:, k, :]).then_inc(x_hi_ready, 1)
                        if k == 0:
                            dve.wait_ge(x_hi_ready, 4 * b + 5)
                            v.tensor_tensor(x_lo[:, k, :], xt_raw[:, k, :], x_hi[:, k, :].bitcast(F32),
                                            ALU.subtract).then_inc(x_lo_ready, 1)
                maxima(b, 3)
                if part != "last":
                    mask_low(b + 1)
                    q_low(b + 1, 0, bank_of("Q0", part))
                if tail:
                    residual(b - 1, 0, part)
                    statistics(b - 1, 0)
                if part != "last":
                    pair_of_steps(b, part)

            pair_of_steps(-1, "lead")
            iteration(0, "first")
            with dve.Fori(1, B - 1) as b:
                iteration(b, "loop")
            iteration(B - 1, "last")
            b = B - 1
            residual(b - 1, 1, "last", (b - 1, 0))
            statistics(b - 1, 1)
            reciprocals(b, (b - 1, 1), chunks=3)
            round_reciprocals(b, 0)
            split_reciprocals(b, 0)
            residual(b - 1, 2, "last")
            normalise(b, 0, "last")
            normalise(b, 1, "last")
            reciprocals(b, second=1)
            round_reciprocals(b, 1)
            residual(b - 1, 3, "last")
            split_reciprocals(b, 1)
            normalise(b, 2, "last")
            statistics(b - 1, 2)
            normalise(b, 3, "last", (b - 1, 2), own=True)
            statistics(b - 1, 3)
            dve.wait_ge(stats_done, 4 * b)
            mean_of(3)
            o_low3(b, x_hi, x_lo)

            def end_statistics(t):
                dve.wait_ge(last_out_done, t + 1)
                v.bn_stats(stats[:, t, :], ps_s[:, t, :]).then_inc(stats_done, 1)

            end_statistics(0)
            dve.wait_ge(stats_done, 4 * b + 1)
            mean_of(0)
            times_gamma(b, 0)
            dve.wait_ge(scaled, 4 * b - 1)
            v.tensor_tensor(y[:, 3, :], y[:, 3, :], gamma_sb[:], ALU.mult).then_inc(end_gamma, 1)
            end_statistics(1)
            dve.wait_ge(end_gamma, 1)
            dve.wait_ge(stats_done, 4 * b + 2)
            v.tensor_tensor(y[:, 3, :], y[:, 3, :], beta_sb[:], ALU.add).then_inc(end_y_ready, 1)
            mean_of(1)
            end_statistics(2)
            dve.wait_ge(stats_done, 4 * b + 3)
            times_gamma(b, 1)
            mean_of(2)
            end_statistics(3)
            dve.wait_ge(stats_done, 4 * b + 4)
            times_gamma(b, 2)
            mean_of(3)
            times_gamma(b, 3)
            for t in (1, 2, 3):
                dve.wait_ge(scaled, 4 * b + t + 1)
                v.tensor_tensor(res_x[:, t, :], res_x[:, t, :], beta_sb[:], ALU.add).then_inc(end_y_ready, 1)

        @block.gpsimd
        def _(pool):
            gp = nc.gpsimd

            def k_blocks(b, c):
                kv = slice(KPC * c, KPC * (c + 1))
                head = const[:, C_HEAD:C_HEAD + GRP].rearrange("p (o g r) -> p o g r", o=1, r=1).broadcast_to([P, KPC, GRP, S])
                for part in range(2):
                    src = k_rep[:, b, part, kv, :] if isinstance(b, int) else \
                        k_rep[:, bass.ds(b, 1), part, kv, :].rearrange("p o h s -> p (o h) s")
                    last = gp.tensor_tensor(k_blk[:, part, kv, :, :],
                                            src.rearrange("p h (o s) -> p h o s", o=1).broadcast_to([P, KPC, GRP, S]),
                                            head, ALU.mult)
                last.then_inc(k_ready, 1)

            def v_blocks(b):
                src = v_rows[:, b, :] if isinstance(b, int) else v_rows[:, bass.ds(b, 1), :].rearrange("p o n -> p (o n)")
                half = const[:, C_HALF:C_HALF + 2].rearrange("p (o h r) -> p o h r", o=1, r=1).broadcast_to([P, KVH, 2, HD])
                gp.tensor_tensor(v_blk[:], src.rearrange("p (k o d) -> p k o d", k=KVH, o=1).broadcast_to([P, KVH, 2, HD]),
                                 half, ALU.mult).then_inc(v_ready, 1)

            def x_low(b, k):
                pool.wait_ge(x_hi_ready, 4 * b + k + 1)
                gp.tensor_tensor(x_lo[:, k, :], xt_raw[:, k, :], x_hi[:, k, :].bitcast(F32), ALU.subtract).then_inc(x_lo_ready, 1)

            def o_low(bt, c, hi=o_hi, lo=o_lo):
                pool.wait_ge(o_hi_ready, 4 * bt + c + 1)
                gp.tensor_tensor(lo[:, c, :], o_sb[:, c, :], hi[:, c, :].bitcast(F32), ALU.subtract).then_inc(o_lo_ready, 1)

            def add_bo(bt, t, place=res_x):
                if place is res_x:
                    pool.wait_ge(res_in[t], 16 * (bt + 2))
                else:
                    pool.wait_ge(last_x_in[t], 16)
                gp.tensor_tensor(place[:, t, :], place[:, t, :], bo_sb[:], ALU.add).then_inc(res_ready, 1)

            def inv_std(bt, t, n=1):
                m = 4 * bt + t + n
                pool.wait_ge(mean_done, m)
                gp.tensor_tensor(var_eps[:, t:t + n], mean_var[:, t:t + n, 1], eps[:, 0:n], ALU.add).then_inc(eps_done, n)
                pool.wait_ge(eps_done, m)
                gp.tensor_tensor(rstd[:, t:t + n], var_eps[:, t:t + n], neg_half[:, 0:n], ALU.pow).then_inc(rstd_done, n)

            def moments(bt, t, n=1):
                m = 4 * bt + t + n
                inv_std(bt, t, n)
                pool.wait_ge(rstd_done, m)
                gp.tensor_tensor(mean_rstd[:, t:t + n], mean_var[:, t:t + n, 0], rstd[:, t:t + n], ALU.mult).then_inc(product_done, n)
                pool.wait_ge(product_done, m)
                gp.tensor_tensor(neg_shift[:, t:t + n], mean_rstd[:, t:t + n], neg_one[:, 0:n], ALU.mult).then_inc(shift_done, n)

            def gamma_beta(bt, t):
                m = 4 * bt + t + 1
                pool.wait_ge(scaled, m)
                gp.tensor_tensor(y[:, t, :], y[:, t, :], gamma_sb[:], ALU.mult).then_inc(gamma_mul, 1)
                pool.wait_ge(gamma_mul, m)
                gp.tensor_tensor(y[:, t, :], y[:, t, :], beta_sb[:], ALU.add).then_inc(y_ready, 1)

            gp.memset(max_cols[:], 0.0).then_inc(zeroed, 1)
            gp.memset(oth_max[:], 0.0).then_inc(zeroed, 1)
            gp.memset(eps[:], EPS).then_inc(zeroed, 1)
            gp.memset(neg_half[:], -0.5).then_inc(zeroed, 1)
            gp.memset(neg_one[:], -1.0).then_inc(zeroed, 1)
            for k in range(NC):
                x_low(0, k)
            pool.wait_ge(early_in, 16)
            for c in range(NC):
                if c % 2 == 0:
                    pool.wait_ge(rep_copied_a, 1 + c // 2)
                    pool.wait_ge(rep_copied_d, 1 + c // 2)
                if c == 2:
                    pool.wait_ge(v_copied, 1)
                    v_blocks(0)
                k_blocks(0, c)
            pool.wait_ge(v_copied, 2)
            pool.wait_ge(zeroed, 5)
            pool.wait_ge(vec_in, 3 * 16)

            def blocks(b, c):
                pool.wait_ge(scores_done, 8 * b + 2 * c + 2)
                k_blocks(b + 1, c)

            def pair_of_steps(b, part):
                tail = part == "loop"
                blocks(b, 2)
                if tail:
                    moments(b - 1, 0)
                    gamma_beta(b - 1, 0)
                pool.wait_ge(pv_done, 4 * b + 4)
                v_blocks(b + 1)
                if tail:
                    moments(b - 1, 1)
                blocks(b, 3)
                if tail:
                    gamma_beta(b - 1, 1)
                    moments(b - 1, 2)
                o_low(b, 0)
                o_low(b, 1)
                if tail:
                    moments(b - 1, 3)
                o_low(b, 2)
                if tail:
                    gamma_beta(b - 1, 2)
                    gamma_beta(b - 1, 3)

            def iteration(b, part):
                tail = part != "first"
                if part == "first":
                    pool.wait_ge(x_lo_ready, 4 * b + 5)
                if part != "last":
                    for k in range(0 if tail else 1, NC):
                        x_low(b + 1, k)
                if tail:
                    add_bo(b - 1, 0)
                if part != "last":
                    blocks(b, 0)
                    blocks(b, 1)
                if tail:
                    for t in (1, 2, 3):
                        add_bo(b - 1, t)
                else:
                    for k in range(NC):
                        pool.wait_ge(wo_hi_ready, k + 1)
                        gp.tensor_tensor(wo_lo[:, k, :], res_x[:, k, :], wo_hi[:, k, :].bitcast(F32),
                                         ALU.subtract).then_inc(wo_lo_ready, 1)
                if part == "last":
                    for t in range(NC):
                        add_bo(b, t, xt_raw)
                else:
                    pair_of_steps(b, part)

            iteration(0, "first")
            with pool.Fori(1, B - 1) as b:
                iteration(b, "loop")
            iteration(B - 1, "last")
            b = B - 1
            moments(b - 1, 0)
            moments(b - 1, 1)
            gamma_beta(b - 1, 0)
            o_low(b, 0, x_hi, x_lo)
            o_low(b, 1, x_hi, x_lo)
            gamma_beta(b - 1, 1)
            o_low(b, 2, x_hi, x_lo)
            moments(b - 1, 2, n=2)
            inv_std(b, 0)
            pool.wait_ge(scaled, 4 * b)
            gamma_beta(b - 1, 2)
            for t in (1, 2, 3):
                inv_std(b, t)
            pool.wait_ge(scaled, 4 * b + 1)
            gp.tensor_tensor(res_x[:, 0, :], res_x[:, 0, :], beta_sb[:], ALU.add).then_inc(y_ready, 1)


def constants():
    c = np.zeros((P, C_ALL), np.float32)
    r = np.arange(P)
    c[r, C_ID + r] = 1
    for j in range(PAIRS):
        for h in range(2):
            for part in range(3):
                c[64 * h + 3 * j + part, C_MAX + j * P + 64 * h:C_MAX + j * P + 64 * (h + 1)] = -1
    for part in range(2):
        for h in range(2):
            c[part * S + np.arange(S), C_MASK + h * S + np.arange(S)] = 1
    for chunk in range(NC):
        for pair in range(PAIRS):
            for h in range(2):
                row, col = BLK * pair + 2 * chunk + h, BLK * pair + HD * h
                for part in range(2):
                    c[row + HPC * part, C_SPREAD + chunk * P + col:C_SPREAD + chunk * P + col + HD] = 1
        for m in range(BLK):
            head = slice(S * (m % 2), S * (m % 2 + 1))
            if m % 8 // 2 == chunk:
                c[head, C_SUM + chunk * BLK + m] = 1
            if m % 8 // 2 >= NC - 2:
                c[head, C_SUM + NC * BLK + m] = 1
            c[head, C_SUM + (NC + 1) * BLK + m] = 1
    for g in range(GRP):
        c[:, C_HEAD + g] = (r % 64) // HD == g
    c[:, C_PART] = np.where(r % BLK // HPC == 1, -1, 0)
    for h in range(2):
        c[:, C_HALF + h] = r // S == h
    return c


def kernel(x, ctx_2048, mask_Bx1xSxS2_ff0, L0_xattn_Wq, L0_xattn_bq, L0_xattn_Wk, L0_xattn_bk, L0_xattn_Wv,
           L0_xattn_bv, L0_xattn_Wo, L0_xattn_bo, L0_xattn_gamma, L0_xattn_beta):
    import concourse.bacc as bacc
    from concourse.bass_utils import run_bass_kernel_spmd

    x = np.asarray(x)
    arrays = {
        "x_t": x.transpose(0, 2, 1).reshape(B, NC, P, L),
        "x_n": x.reshape(B * L, D),
        "ctx_t": np.asarray(ctx_2048).reshape(B, S, NC, P).transpose(3, 2, 0, 1).reshape(P, NC, B * S),
        "mask_t": np.asarray(mask_Bx1xSxS2_ff0).reshape(B, L, S).transpose(0, 2, 1),
        "wq": np.asarray(L0_xattn_Wq),
        "bq": np.asarray(L0_xattn_bq).reshape(NC, P).T,
        "wk": np.asarray(L0_xattn_Wk),
        "bk": np.asarray(L0_xattn_bk).reshape(P, 1),
        "wv": np.asarray(L0_xattn_Wv),
        "bv": np.asarray(L0_xattn_bv),
        "wo": np.asarray(L0_xattn_Wo),
        "bo": np.asarray(L0_xattn_bo),
        "gamma": np.asarray(L0_xattn_gamma),
        "beta": np.asarray(L0_xattn_beta),
        "consts": constants(),
    }
    arrays = {name: np.ascontiguousarray(a) for name, a in arrays.items()}
    nc = bacc.Bacc("TRN2", target_bir_lowering=False, num_devices=1)
    args = {name: nc.dram_tensor(name, a.shape, mybir.dt.from_np(a.dtype), kind="ExternalInput").ap()
            for name, a in arrays.items()}
    out = nc.dram_tensor("out", (B * L, D), F32, kind="ExternalOutput").ap()
    cross_attention(nc, out=out, **args)
    result = run_bass_kernel_spmd(nc, [arrays], core_ids=[0])
    return result.results[0]["out"].reshape(B, L, D)
```
